# Optimizing a Trainium2 kernel written in Bass

```python
import numpy as np
import jax
import jax.numpy as jnp

def _softmax(x, axis=-1):
    return jax.nn.softmax(x, axis=axis)

def _gelu(x):
    return jax.nn.gelu(x, approximate=True)

def _silu(x):
    return jax.nn.silu(x)

def _sigmoid(x):
    return jax.nn.sigmoid(x)

def _layernorm(x, axis=-1, eps=1e-05):
    m = jnp.mean(x, axis=axis, keepdims=True)
    v = jnp.var(x, axis=axis, keepdims=True)
    return (x - m) / jnp.sqrt(v + eps)

def _scatter_add(tgt, idx, src, axis=0):
    return tgt.at[idx].add(src)

def _segment_sum(src, seg, n):
    return jax.ops.segment_sum(src, seg, n)
kernel_name = 'mk_adj_resnorm_d1_adj_r2_e8f7cf'

def setup_inputs(seed: int=0):
    np.random.seed(seed)
    _w = jnp.asarray

    def _rec_inputs():
        import jax
        import jax.numpy as jnp
        _gk = jax.random.key(seed)
        x = -0.0001538 + 1 * jax.random.normal(jax.random.fold_in(_gk, 1), (32, 256, 384), jnp.float32)
        _a = jax.random.bernoulli(jax.random.fold_in(_gk, 2), 0.0625, (32, 256, 256))
        _a = jnp.logical_or(_a, jnp.swapaxes(_a, -1, -2))
        _a = jnp.logical_or(_a, jnp.eye(256, dtype=bool))
        _af = _a.astype(jnp.float32)
        _af = _af * jax.random.uniform(jax.random.fold_in(_gk, 3), (32, 256, 256), jnp.float32, 0.05, 5.06092)
        adj = _af
        return (x, adj)
    x, adj = _rec_inputs()

    def _L0_gnn_setup():
        import jax, jax.numpy as jnp
        import numpy as np
        D_MODEL = 384
        NHEADS = 8
        D_FF = 1536
        B, N = (8, 512)
        EPS = 1e-06

        def _rmsnorm(x, alpha, gamma):
            x = x * jax.lax.rsqrt(jnp.mean(x * x, axis=-1, keepdims=True) + EPS)
            return alpha * x + gamma
        key = jax.random.key(seed)
        ks = jax.random.split(key, 10)
        d, f = (D_MODEL, D_FF)
        s = 1.0 / np.sqrt(d)
        inp = {'x': jax.random.normal(ks[0], (B, N, d), dtype=jnp.float32), 'attn_bias': jax.random.normal(ks[1], (B, N, N), dtype=jnp.float32), 'wq': jax.random.normal(ks[2], (d, d), dtype=jnp.float32) * s, 'bq': jnp.zeros((d,), jnp.float32), 'wk': jax.random.normal(ks[3], (d, d), dtype=jnp.float32) * s, 'bk': jnp.zeros((d,), jnp.float32), 'wv': jax.random.normal(ks[4], (d, d), dtype=jnp.float32) * s, 'bv': jnp.zeros((d,), jnp.float32), 'wo': jax.random.normal(ks[5], (d, d), dtype=jnp.float32) * s, 'bo': jnp.zeros((d,), jnp.float32), 'w1': jax.random.normal(ks[6], (d, f), dtype=jnp.float32) * s, 'b1': jnp.zeros((f,), jnp.float32), 'w2': jax.random.normal(ks[7], (f, d), dtype=jnp.float32) * (1.0 / np.sqrt(f)), 'b2': jnp.zeros((d,), jnp.float32), 'alpha1': jnp.ones((d,), jnp.float32), 'gamma1': jnp.ones((d,), jnp.float32), 'alpha2': jnp.ones((d,), jnp.float32), 'gamma2': jnp.ones((d,), jnp.float32)}
        return inp
    _L0_gnn_all = _L0_gnn_setup()
    _L0_gnn_in = {k: v for k, v in _L0_gnn_all.items() if k in ('wq', 'bq', 'wk', 'bk', 'wv', 'bv', 'wo', 'bo', 'w1', 'b1', 'w2', 'b2', 'alpha1', 'gamma1', 'alpha2', 'gamma2')}
    del _L0_gnn_all
    return {'x': x, 'adj': adj, 'L0_gnn_wq': _L0_gnn_in['wq'], 'L0_gnn_bq': _L0_gnn_in['bq'], 'L0_gnn_wk': _L0_gnn_in['wk'], 'L0_gnn_bk': _L0_gnn_in['bk'], 'L0_gnn_wv': _L0_gnn_in['wv'], 'L0_gnn_bv': _L0_gnn_in['bv'], 'L0_gnn_wo': _L0_gnn_in['wo'], 'L0_gnn_bo': _L0_gnn_in['bo'], 'L0_gnn_w1': _L0_gnn_in['w1'], 'L0_gnn_b1': _L0_gnn_in['b1'], 'L0_gnn_w2': _L0_gnn_in['w2'], 'L0_gnn_b2': _L0_gnn_in['b2'], 'L0_gnn_alpha1': _L0_gnn_in['alpha1'], 'L0_gnn_gamma1': _L0_gnn_in['gamma1'], 'L0_gnn_alpha2': _L0_gnn_in['alpha2'], 'L0_gnn_gamma2': _L0_gnn_in['gamma2']}

def reference(x, adj, L0_gnn_wq, L0_gnn_bq, L0_gnn_wk, L0_gnn_bk, L0_gnn_wv, L0_gnn_bv, L0_gnn_wo, L0_gnn_bo, L0_gnn_w1, L0_gnn_b1, L0_gnn_w2, L0_gnn_b2, L0_gnn_alpha1, L0_gnn_gamma1, L0_gnn_alpha2, L0_gnn_gamma2):
    import jax
    import jax.numpy as jnp

    def _L0_gnn_ref(x, attn_bias, wq, bq, wk, bk, wv, bv, wo, bo, w1, b1, w2, b2, alpha1, gamma1, alpha2, gamma2):
        import jax, jax.numpy as jnp
        import numpy as np
        D_MODEL = 384
        NHEADS = 8
        D_FF = 1536
        B, N = (8, 512)
        EPS = 1e-06

        def _rmsnorm(x, alpha, gamma):
            x = x * jax.lax.rsqrt(jnp.mean(x * x, axis=-1, keepdims=True) + EPS)
            return alpha * x + gamma
        b, n, d = x.shape
        h = NHEADS
        dh = d // h
        scaling = dh ** (-0.5)

        def split_heads(t):
            return t.reshape(b, n, h, dh).transpose(0, 2, 1, 3)
        q = split_heads(x @ wq + bq)
        k = split_heads(x @ wk + bk)
        v = split_heads(x @ wv + bv)
        scores = jnp.einsum('bhqd,bhkd->bhqk', q, k) * scaling
        scores = scores + attn_bias[:, None, :, :]
        attn = jax.nn.softmax(scores, axis=-1)
        ctx = jnp.einsum('bhij,bhjd->bhid', attn, v)
        ctx = ctx.transpose(0, 2, 1, 3).reshape(b, n, d)
        attn_out = ctx @ wo + bo
        x = _rmsnorm(x + attn_out, alpha1, gamma1)
        ff = jax.nn.silu(x @ w1 + b1) @ w2 + b2
        x = _rmsnorm(x + ff, alpha2, gamma2)
        return x
    x = _layernorm(x + _L0_gnn_ref(x, adj, L0_gnn_wq, L0_gnn_bq, L0_gnn_wk, L0_gnn_bk, L0_gnn_wv, L0_gnn_bv, L0_gnn_wo, L0_gnn_bo, L0_gnn_w1, L0_gnn_b1, L0_gnn_w2, L0_gnn_b2, L0_gnn_alpha1, L0_gnn_gamma1, L0_gnn_alpha2, L0_gnn_gamma2), axis=-1)
    return x

_drawn_inputs = setup_inputs


def setup_inputs(seed=0):
    import zlib

    import numpy as np

    out = dict(_drawn_inputs(seed))
    spreads = {'L0_gnn_bq': (0.0, 0.756),
     'L0_gnn_bk': (0.0, 0.8),
     'L0_gnn_bv': (0.0, 0.1),
     'L0_gnn_bo': (0.0, 0.1),
     'L0_gnn_b1': (0.0, 0.339),
     'L0_gnn_b2': (0.0, 0.1),
     'L0_gnn_alpha1': (1.0, 0.2),
     'L0_gnn_gamma1': (1.0, 0.2),
     'L0_gnn_alpha2': (1.0, 0.2),
     'L0_gnn_gamma2': (1.0, 0.2)}
    factors = {}
    for name, (base, spread) in spreads.items():
        noise = np.random.default_rng([zlib.crc32(name.encode()), seed]).standard_normal(out[name].shape)
        drawn = base * np.exp(spread * noise) if base else spread * noise
        out[name] = jnp.asarray(drawn.astype(out[name].dtype))
    for name, factor in factors.items():
        out[name] = (out[name] * factor).astype(out[name].dtype)
    return out
```

```python
from contextlib import ExitStack

import concourse.bass as bass
from concourse import mybir

F32 = mybir.dt.float32
F32R = mybir.dt.float32r
ALU = mybir.AluOpType
ACT = mybir.ActivationFunctionType

P = 128
RMS_EPS = 1e-6
LN_EPS = 1e-5


def resnorm_kernel(nc, x, x_t, adj, wq, bq, wk, bk, wv, bv, wo, bo, w1, b1, w2, b2,
                   alpha1, gamma1, alpha2, gamma2, out):
    B, N, D = x.shape
    F = w1.shape[1]
    H = 8
    DH = D // H
    NPAIR = H // 2
    PW = 64 + DH
    KT = D // P
    FT = F // P
    BPB = 2
    TB = BPB * N
    NT = TB // P
    QT = N // P
    NBLK = B // BPB
    STEPS = H * BPB
    LAST = STEPS + 3
    SCALE = float(DH) ** -0.5
    QK0, VP, QKP = 2, NT, 2 * (NPAIR - 1)
    PROJ = QK0 + VP + QKP
    assert N == 256 and D == 384 and B % BPB == 0 and PROJ % 2 == 0

    xf = x.rearrange("b n d -> (b n) d")
    outf = out.rearrange("b n d -> (b n) d")
    adj_v = adj.rearrange("b (t p) k -> p (b t) k", p=P)

    with ExitStack() as ctx:
        cursor = [nc.sbuf_base + (-nc.sbuf_base) % 64]

        def put(name, shape, dt=F32, at=None):
            size = 4
            for n in shape[1:]:
                size *= n
            if at is None:
                at = cursor[0]
                cursor[0] += size + (-size) % 32
            return nc.alloc_sbuf_tensor_at(name, shape, dt, offset=at)

        def sem(name):
            return ctx.enter_context(nc.semaphore(name))

        wq_h, wq_l, wk_h, wk_l = [put(n, [P, KT, NPAIR * PW], F32R) for n in ("wq_h", "wq_l", "wk_h", "wk_l")]
        wv_h, wv_l = put("wv_h", [P, KT, D], F32R), put("wv_l", [P, KT, D], F32R)
        wo_h, wo_l = put("wo_h", [P, NPAIR, D], F32R), put("wo_l", [P, NPAIR, D], F32R)
        w1_h, w1_l = put("w1_h", [P, KT, F], F32R), put("w1_l", [P, KT, F], F32R)
        w2_h, w2_l = put("w2_h", [P, FT, D], F32R), put("w2_l", [P, FT, D], F32R)
        bo_bc, gb2_bc, a1_bc, a2_bc, g2_bc = [
            put(n, [P, D]) for n in ("bo_bc", "gb2_bc", "a1_bc", "a2_bc", "g2_bc")]
        ident = put("ident", [P, P])
        nbq, bkc, bvc = put("nbq", [P, NPAIR]), put("bkc", [P, NPAIR]), put("bvc", [P, NPAIR])
        g1c, hb1 = put("g1c", [P, KT]), put("hb1", [P, FT])
        mhalf = put("mhalf", [P, 1])
        nmax, rsum, rrec = [put(n, [P, STEPS * QT]) for n in ("nmax", "rsum", "rrec")]
        ss1, ms1, r1 = [put(n, [P, NT]) for n in ("ss1", "ms1", "r1")]
        ss2, ms2, r2 = [put(n, [P, NT]) for n in ("ss2", "ms2", "r2")]
        sw, nmean, sv, msv, rstd = [put(n, [P, NT]) for n in ("sw", "nmean", "sv", "msv", "rstd")]
        v_h, v_l = put("v_h", [P, NT, D], F32R), put("v_l", [P, NT, D], F32R)
        nadj = put("nadj", [P, NT, N])
        xt_raw = put("xt_raw", [P, KT, TB])
        xt_h, xt_l = put("xt_h", [P, KT, TB], F32R), put("xt_l", [P, KT, TB], F32R)
        xb = put("xb", [P, NT, D])
        xg = put("xg", [P, 2, D])
        x1 = put("x1", [P, NT, D])
        junk = put("junk", [P, D])
        qh0, ql0, kh0, kl0 = [put(n, [P, TB], F32R) for n in ("qh0", "ql0", "kh0", "kl0")]
        over_ctx = cursor[0]
        ctx_h, ctx_l = put("ctx_h", [P, NPAIR, TB], F32R), put("ctx_l", [P, NPAIR, TB], F32R)
        g_h = put("g_h", [P, 4, TB], F32R, at=over_ctx)
        g_l = put("g_l", [P, 4, TB], F32R, at=over_ctx + 4 * TB * 4)
        over_att = cursor[0]
        qh1, ql1, kh1, kl1 = [put(n, [P, TB], F32R) for n in ("qh1", "ql1", "kh1", "kl1")]
        prob = put("prob", [P, 3, QT * N])
        pt_h, pt_l = put("pt_h", [P, 2, TB], F32R), put("pt_l", [P, 2, TB], F32R)
        row = TB * 4
        x1t_h = put("x1t_h", [P, KT, TB], F32R, at=over_att)
        x1t_l = put("x1t_l", [P, KT, TB], F32R, at=over_att + KT * row)
        tnh = put("tnh", [P, 2, TB], at=over_att + 2 * KT * row)
        sil = put("sil", [P, 2, TB], at=over_att + (2 * KT + 2) * row)
        STAGE = 1536
        stage = [put(f"stage{n}", [P, STAGE], at=over_ctx + n * STAGE * 4) for n in range(6)]
        qh, ql, kh, kl = (qh0, qh1), (ql0, ql1), (kh0, kh1), (kl0, kl1)

        psum = ctx.enter_context(nc.psum_tensor("psum", [P, 8, 512], F32))
        PROJ_BANK, SCORE_BANK, PT_BANK, CTX_BANK = (0, 1), (2, 3), (4, 5), (6, 7)
        WO_BANK = (2, 3, 4, 5)
        X1T_BANK = (6, 7, 2)
        F1_BANK = (2, 3)
        F2_BANK = (4, 5, 6, 7)

        NCHUNK = 10
        w_in = [sem(f"w_in{n}") for n in range(NCHUNK)]
        const_in = sem("const_in")
        xt_in = [sem(f"xt_in{k}") for k in range(KT)]
        adj_in = sem("adj_in")
        xb_in = [sem(f"xb_in{t}") for t in range(NT)]
        xg_in = [sem(f"xg_in{t}") for t in range(2)]
        out_dma = [sem(f"out_dma{t}") for t in range(NT)]
        dve_past, pool_past = sem("dve_past"), sem("pool_past")
        zero_done = sem("zero_done")
        const_done = sem("const_done")
        ident_done = sem("ident_done")
        scaled = sem("scaled")
        wh_done = sem("wh_done")
        wl_done = sem("wl_done")
        proj_done = sem("proj_done")
        sc_done = sem("sc_done")
        pt_done = sem("pt_done")
        av_done = sem("av_done")
        wo_done = sem("wo_done")
        x1t_done = sem("x1t_done")
        f1_done = sem("f1_done")
        f2_step = sem("f2_step")
        f2_done = sem("f2_done")
        proj_h = sem("proj_h")
        pt_hi = sem("pt_hi")
        exp_done = sem("exp_done")
        ctx_hi = sem("ctx_hi")
        sq1_done = sem("sq1_done")
        x1t_hi = sem("x1t_hi")
        tz_done = sem("tz_done")
        g_hi = sem("g_hi")
        sq2_done = sem("sq2_done")
        var_done = sem("var_done")
        proj_l = sem("proj_l")
        max_done = sem("max_done")
        rec_done = sem("rec_done")
        pt_lo = sem("pt_lo")
        ctx_lo = sem("ctx_lo")
        t1_done = sem("t1_done")
        x1_done = sem("x1_done")
        x1t_lo = sem("x1t_lo")
        g_done = sem("g_done")
        g_lo = sem("g_lo")
        z_done = sem("z_done")
        w_done = sem("w_done")
        out_done = sem("out_done")
        prob_done = sem("prob_done")
        nadj_done = sem("nadj_done")
        xt_done = sem("xt_done")
        xt_hi = sem("xt_hi")
        xb_done = sem("xb_done")
        xg_done = sem("xg_done")
        ms1_done = sem("ms1_done")
        r1_done = sem("r1_done")
        x1b_done = sem("x1b_done")
        ms2_done = sem("ms2_done")
        r2_done = sem("r2_done")
        za_done = sem("za_done")
        nmean_done = sem("nmean_done")
        msv_done = sem("msv_done")
        rstd_done = sem("rstd_done")

        def since(eng, semaphore, count):
            if not (isinstance(count, int) and count <= 0):
                eng.wait_ge(semaphore, count)

        chunks = [("wq", 0), ("wk", 0), ("wv", 0), ("wo", 0)] + [("w1", k) for k in range(KT)] \
            + [("w2", k) for k in range(FT // 4)]
        assert len(chunks) == NCHUNK

        def stage_of(c):
            return stage[c % len(stage)]

        def chunk_parts(c):
            name, k = chunks[c]
            s = stage_of(c)
            if name in ("wq", "wk"):
                h, l = (wq_h, wq_l) if name == "wq" else (wk_h, wk_l)
                parts = []
                for kk in range(KT):
                    for a in range(2):
                        src = s[:, kk * D:(kk + 1) * D].rearrange("p (r a d) -> p r a d", r=NPAIR, a=2)[:, :, a, :]
                        dst = [w[:, kk, :].rearrange("p (r c) -> p r c", r=NPAIR)[:, :, 64 * a:64 * a + DH]
                               for w in (h, l)]
                        parts.append((src, *dst))
                return parts
            if name == "wv":
                return [(s[:, 0:KT * D].rearrange("p (k n) -> p k n", k=KT), wv_h[:, :, :], wv_l[:, :, :])]
            if name == "wo":
                v = s[:, 0:NPAIR * D].rearrange("p (r n) -> p r n", r=NPAIR)
                return [(v[64 * a:64 * a + DH], wo_h[64 * a:64 * a + DH, :, :], wo_l[64 * a:64 * a + DH, :, :])
                        for a in range(2)]
            if name == "w1":
                return [(s[:, 0:F], w1_h[:, k, :], w1_l[:, k, :])]
            v = s[:, 0:4 * D].rearrange("p (g n) -> p g n", g=4)
            return [(v, w2_h[:, 4 * k:4 * k + 4, :], w2_l[:, 4 * k:4 * k + 4, :])]

        pair_biases = [(bq, nbq), (bk, bkc), (bv, bvc)]
        NCONST = 2 * len(pair_biases) + 2 + 6

        block = ctx.enter_context(nc.Block())

        @block.sync
        def _(sp):
            def load_chunk(c):
                name, k = chunks[c]
                s = stage_of(c)
                if c >= len(stage):
                    sp.wait_ge(wl_done, c - len(stage) + 1)
                if name in ("wq", "wk", "wv"):
                    w = {"wq": wq, "wk": wk, "wv": wv}[name]
                    sp.dma_start(s[:, 0:KT * D].rearrange("p (k n) -> p k n", k=KT),
                                 w.rearrange("(k p) n -> p k n", p=P)).then_inc(w_in[c], 16)
                elif name == "wo":
                    v = s[:, 0:NPAIR * D].rearrange("p (r n) -> p r n", r=NPAIR)
                    src = wo.rearrange("(r a d) n -> a d r n", r=NPAIR, a=2)
                    for a in range(2):
                        sp.dma_start(v[64 * a:64 * a + DH], src[a]).then_inc(w_in[c], 16)
                elif name == "w1":
                    sp.dma_start(s[:, 0:F], w1[k * P:(k + 1) * P, :]).then_inc(w_in[c], 16)
                else:
                    sp.dma_start(s[:, 0:4 * D].rearrange("p (g n) -> p g n", g=4),
                                 w2[4 * k * P:4 * (k + 1) * P, :].rearrange("(g p) n -> p g n", p=P)
                                 ).then_inc(w_in[c], 16)

            def load_xt(i, k):
                sp.dma_start(xt_raw[:, k, :], x_t[k * P:(k + 1) * P, bass.ds(i * TB, TB)]).then_inc(xt_in[k], 16)

            def load_adj(i):
                sp.dma_start(nadj[:, :, :], adj_v[:, bass.ds(i * NT, NT), :]).then_inc(adj_in, 16)

            def load_x(dst, i, t, arrived):
                sp.dma_start(dst, xf[bass.ds(i * TB + t * P, P), :]).then_inc(arrived, 16)

            def loads_and_stores(i, tail, more):
                if tail:
                    j = i - 1
                    for t in range(NT):
                        if t < 2:
                            sp.wait_ge(w_done, j * NT + t + 1)
                            load_x(xg[:, t, :], j, t + 2, xg_in[t])
                    for t in range(NT):
                        sp.wait_ge(out_done, j * NT + t + 1)
                        sp.dma_start(outf[bass.ds(j * TB + t * P, P), :], x1[:, t, :]).then_inc(out_dma[t], 16)
                for t in range(NT):
                    since(sp, t1_done, i * NT - NT + t + 1)
                    load_x(xb[:, t, :], i, t, xb_in[t])
                if more:
                    for k in range(KT):
                        sp.wait_ge(xt_done, i * KT + k + 1)
                        load_xt(i + 1, k)
                    sp.wait_ge(max_done, i * (STEPS * QT) + STEPS * QT)
                    load_adj(i + 1)
                for t in range(2):
                    since(sp, w_done, i * NT - NT + t + 3)
                    load_x(xg[:, t, :], i, t, xg_in[t])

            load_chunk(0)
            load_chunk(1)
            for k in range(KT):
                load_xt(0, k)
            load_chunk(2)
            sp.wait_ge(zero_done, 1)
            for dram, tile in pair_biases:
                src = dram.rearrange("(r a d) -> a d r", r=NPAIR, a=2)
                for a in range(2):
                    sp.dma_start(tile[64 * a:64 * a + DH, :], src[a], allow_slow_non_contiguous=True).then_inc(const_in, 16)
            sp.dma_start(g1c[:, :], gamma1.rearrange("(k p) -> p k", p=P), allow_slow_non_contiguous=True).then_inc(const_in, 16)
            sp.dma_start(hb1[:, :], b1.rearrange("(f p) -> p f", p=P), allow_slow_non_contiguous=True).then_inc(const_in, 16)
            for tile, dram in ((bo_bc, bo), (gb2_bc, gamma1), (a1_bc, alpha1), (a2_bc, alpha2),
                               (g2_bc, gamma2), (junk, b2)):
                sp.dma_start(tile[:, :], dram.partition_broadcast(P)).then_inc(const_in, 16)
            load_adj(0)
            for c in range(3, NCHUNK):
                load_chunk(c)

            loads_and_stores(0, tail=False, more=True)
            with sp.Fori(1, NBLK - 1) as i:
                loads_and_stores(i, tail=True, more=True)
            loads_and_stores(NBLK - 1, tail=True, more=False)
            j = NBLK - 1
            for t in range(2):
                sp.wait_ge(w_done, j * NT + t + 1)
                load_x(xg[:, t, :], j, t + 2, xg_in[t])
            for t in range(NT):
                sp.wait_ge(out_done, j * NT + t + 1)
                sp.dma_start(outf[j * TB + t * P:j * TB + (t + 1) * P, :], x1[:, t, :]).then_inc(out_dma[t], 16)
            for t in range(NT):
                sp.wait_ge(out_dma[t], 16 * NBLK)

        @block.gpsimd
        def _(pool):
            def split_xt(i, k):
                pool.wait_ge(xt_in[k], i * 16 + 16)
                since(pool, proj_done, i * PROJ)
                pool.sem_inc(pool_past, 1)
                pool.tensor_scalar(xt_h[:, k, :], xt_raw[:, k, :], 1.0, 0.0, ALU.mult, ALU.add).then_inc(xt_hi, 1)
                pool.wait_ge(xt_hi, i * KT + k + 1)
                pool.tensor_tensor(xt_l[:, k, :], xt_raw[:, k, :], xt_h[:, k, :].bitcast(F32),
                                   ALU.subtract).then_inc(xt_done, 1)

            def negate_adj(i):
                pool.wait_ge(adj_in, i * 16 + 16)
                pool.sem_inc(pool_past, 1)
                pool.tensor_scalar(nadj[:, :, :], nadj[:, :, :], -1.0, 0.0, ALU.mult, ALU.add).then_inc(nadj_done, 1)

            def normalise(i, s):
                pool.wait_ge(rec_done, i * STEPS + s + 1)
                pool.sem_inc(pool_past, 1)
                for q in range(QT):
                    c = s * QT + q
                    last = pool.tensor_scalar(prob[:, s % 3, q * N:(q + 1) * N], prob[:, s % 3, q * N:(q + 1) * N],
                                              rrec[:, c:c + 1], 0.0, ALU.mult, ALU.add)
                last.then_inc(prob_done, 1)

            def add_xb(i, t):
                pool.wait_ge(xb_in[t], i * 16 + 16)
                pool.tensor_tensor(xb[:, t, :], xb[:, t, :], bo_bc[:, :], ALU.add).then_inc(xb_done, 1)

            def add_xg(j, t):
                pool.wait_ge(xg_in[t % 2], j * 32 + 16 * (t // 2) + 16)
                pool.tensor_tensor(xg[:, t % 2, :], xg[:, t % 2, :], g2_bc[:, :], ALU.add).then_inc(xg_done, 1)

            def rsqrt_mean(sums, mean, root, t, eps, mean_done, root_done, count):
                pool.sem_inc(pool_past, 1)
                pool.tensor_scalar(mean[:, t:t + 1], sums[:, t:t + 1], 1.0 / D, eps, ALU.mult, ALU.add)\
                    .then_inc(mean_done, 1)
                pool.wait_ge(mean_done, count)
                pool.tensor_tensor(root[:, t:t + 1], mean[:, t:t + 1], mhalf[:, 0:1], ALU.pow).then_inc(root_done, 1)

            def norm1_root(i, t):
                pool.wait_ge(sq1_done, i * NT + t + 1)
                rsqrt_mean(ss1, ms1, r1, t, RMS_EPS, ms1_done, r1_done, i * NT + t + 1)

            def add_b2(i, t):
                pool.wait_ge(x1t_done, i * KT + KT)
                pool.tensor_tensor(x1[:, t, :], x1[:, t, :], gb2_bc[:, :], ALU.add).then_inc(x1b_done, 1)

            def norm2_root(j, t):
                pool.wait_ge(sq2_done, j * NT + t + 1)
                rsqrt_mean(ss2, ms2, r2, t, RMS_EPS, ms2_done, r2_done, j * NT + t + 1)
                pool.tensor_tensor(x1[:, t, :], x1[:, t, :], a2_bc[:, :], ALU.mult).then_inc(za_done, 1)

            def layer_mean(j, t):
                pool.wait_ge(w_done, j * NT + t + 1)
                pool.sem_inc(pool_past, 1)
                pool.tensor_scalar(nmean[:, t:t + 1], sw[:, t:t + 1], -1.0 / D, 0.0, ALU.mult, ALU.add)\
                    .then_inc(nmean_done, 1)

            def layer_root(j, t):
                pool.wait_ge(var_done, j * NT + t + 1)
                rsqrt_mean(sv, msv, rstd, t, LN_EPS, msv_done, rstd_done, j * NT + t + 1)

            def tail_step(j, s):
                if s == 0:
                    norm2_root(j, 0)
                if s == 1:
                    norm2_root(j, 1)
                    norm2_root(j, 2)
                if s == 2:
                    norm2_root(j, 3)
                if s in (4, 5):
                    add_xg(j, s - 2)
                if s in (3, 4, 6, 7):
                    layer_mean(j, {3: 0, 4: 1, 6: 2, 7: 3}[s])
                if s in (4, 5, 7, 8):
                    layer_root(j, {4: 0, 5: 1, 7: 2, 8: 3}[s])

            def work(i, tail, more):
                for s in range(STEPS):
                    if tail:
                        tail_step(i - 1, s)
                    if 9 <= s < 9 + NT and s < 13:
                        add_xb(i, s - 9)
                    if more and s in (13, 14, 15):
                        split_xt(i + 1, s - 13)
                    normalise(i, s)
                for t in range(NT):
                    norm1_root(i, t)
                for t in range(NT):
                    add_b2(i, t)
                if more:
                    negate_adj(i + 1)
                for t in range(2):
                    add_xg(i, t)

            pool.memset(ident[:, :], 0.0).then_inc(ident_done, 1)
            pool.memset(mhalf[:, :], -0.5)
            pool.wait_ge(ident_done, 1)
            pool.affine_select(out=ident[:, :], in_=ident[:, :], compare_op=ALU.not_equal, fill=1.0, base=0,
                               pattern=[[-1, P]], channel_multiplier=1).then_inc(ident_done, 1)
            pool.wait_ge(w_in[0], 16)
            pool.tensor_scalar(stage[0][:, 0:KT * D], stage[0][:, 0:KT * D], -SCALE, 0.0, ALU.mult, ALU.add)\
                .then_inc(scaled, 1)
            for k in range(KT):
                split_xt(0, k)
            pool.wait_ge(const_in, 16 * NCONST)
            pool.tensor_scalar(nbq[:, :], nbq[:, :], -SCALE, 0.0, ALU.mult, ALU.add)
            pool.tensor_scalar(hb1[:, :], hb1[:, :], 0.5, 0.0, ALU.mult, ALU.add)
            pool.tensor_tensor(gb2_bc[:, :], gb2_bc[:, :], junk[:, :], ALU.add).then_inc(const_done, 1)
            negate_adj(0)

            work(0, tail=False, more=True)
            with pool.Fori(1, NBLK - 1) as i:
                work(i, tail=True, more=True)
            work(NBLK - 1, tail=True, more=False)
            for s in range(9):
                tail_step(NBLK - 1, s)

        @block.scalar
        def _(act):
            def proj_high(n, bank, dst, bias=None):
                act.wait_ge(proj_done, n + 1)
                src = psum[0:dst.shape[0], bank, 0:dst.shape[1]]
                if bias is None:
                    act.activation(dst, src, ACT.Copy).then_inc(proj_h, 1)
                else:
                    act.activation(dst, src, ACT.Identity, bias=bias).then_inc(proj_h, 1)

            def qk_high(i, p, which):
                n = i * PROJ + (which if p == 0 else QK0 + VP + 2 * (p - 1) + which)
                since(act, sc_done, i * STEPS + 4 * (p - 1))
                proj_high(n, PROJ_BANK[which], (qh, kh)[which][p % 2][0:PW, :], (nbq, bkc)[which][0:PW, p:p + 1])

            def v_high(i, t):
                since(act, av_done, i * STEPS)
                proj_high(i * PROJ + QK0 + t, PROJ_BANK[t % 2], v_h[:, t, :])

            def exponentials(i, s):
                for q in range(QT):
                    c = s * QT + q
                    act.wait_ge(max_done, i * (STEPS * QT) + c + 1)
                    part = prob[:, s % 3, q * N:(q + 1) * N]
                    act.activation(part, part, ACT.Exp, bias=nmax[:, c:c + 1], scale=-1.0,
                                   accum_out=rsum[:, c:c + 1]).then_inc(exp_done, 1)

            def pt_high(i, s):
                act.wait_ge(pt_done, i * STEPS + s + 1)
                since(act, av_done, i * STEPS + s - 1)
                act.activation(pt_h[:, s % 2, :], psum[:, PT_BANK[s % 2], :], ACT.Copy).then_inc(pt_hi, 1)

            def ctx_high(i, hd):
                p, a = hd // 2, hd % 2
                m = 64 if a == 0 else DH
                act.wait_ge(av_done, i * STEPS + 2 * hd + 2)
                act.activation(ctx_h[64 * a:64 * a + m, p, :], psum[0:m, CTX_BANK[hd % 2], :], ACT.Identity,
                               bias=bvc[64 * a:64 * a + m, p:p + 1]).then_inc(ctx_hi, 1)

            def square1(i, t):
                act.wait_ge(t1_done, i * NT + t + 1)
                act.activation(psum[:, WO_BANK[t], 0:D], x1[:, t, :], ACT.Square,
                               accum_out=ss1[:, t:t + 1]).then_inc(sq1_done, 1)

            def x1t_high(i, k):
                act.wait_ge(x1t_done, i * KT + k + 1)
                act.activation(x1t_h[:, k, :], psum[:, X1T_BANK[k], :], ACT.Identity,
                               bias=g1c[:, k:k + 1]).then_inc(x1t_hi, 1)

            def silu_terms(i, f):
                act.wait_ge(f1_done, i * FT + f + 1)
                if f >= 2:
                    act.wait_ge(g_lo, i * FT + f - 1)
                src = psum[:, F1_BANK[f % 2], :]
                act.activation(tnh[:, f % 2, :], src, ACT.Tanh, bias=hb1[:, f:f + 1], scale=0.5)
                act.activation(sil[:, f % 2, :], src, ACT.Identity, bias=hb1[:, f:f + 1], scale=0.5)\
                    .then_inc(tz_done, 1)

            def hidden_high(i, f):
                act.wait_ge(g_done, i * FT + f + 1)
                if f >= 4:
                    act.wait_ge(f2_step, i * 8 + f - 3)
                act.activation(g_h[:, f % 4, :], sil[:, f % 2, :], ACT.Copy).then_inc(g_hi, 1)

            def square2(j, t):
                act.wait_ge(z_done, j * NT + t + 1)
                act.activation(psum[:, F2_BANK[t], 0:D], x1[:, t, :], ACT.Square,
                               accum_out=ss2[:, t:t + 1]).then_inc(sq2_done, 1)

            def variance(j, t):
                act.wait_ge(nmean_done, j * NT + t + 1)
                since(act, var_done, j * NT + t)
                act.activation(junk[:, :], x1[:, t, :], ACT.Square, bias=nmean[:, t:t + 1],
                               accum_out=sv[:, t:t + 1]).then_inc(var_done, 1)

            def tail_step(j, s):
                if s == 0:
                    for t in range(NT):
                        square2(j, t)
                if s in (4, 5, 7, 8):
                    variance(j, {4: 0, 5: 1, 7: 2, 8: 3}[s])

            def work(i, tail, more):
                for s in range(LAST + 1):
                    if tail:
                        tail_step(i - 1, s)
                    p = s // 4 + 1
                    if p < NPAIR and s % 4 in (2, 3):
                        qk_high(i, p, s % 4 - 2)
                    if more and s in (17, 18):
                        qk_high(i + 1, 0, s - 17)
                    if s % 2 == 1 and 5 <= s <= LAST:
                        ctx_high(i, (s - 5) // 2)
                    if 2 <= s < STEPS + 2:
                        pt_high(i, s - 2)
                    if s < STEPS:
                        exponentials(i, s)
                for t in range(NT):
                    square1(i, t)
                if more:
                    for t in range(NT - 1):
                        v_high(i + 1, t)
                for k in range(KT):
                    x1t_high(i, k)
                if more:
                    v_high(i + 1, NT - 1)
                for f in range(FT):
                    silu_terms(i, f)
                    hidden_high(i, f)

            act.wait_ge(zero_done, 1)
            for c in range(NCHUNK):
                act.wait_ge(w_in[c], 32 if chunks[c][0] == "wo" else 16)
                if c == 0:
                    act.wait_ge(scaled, 1)
                for staged, high, _ in chunk_parts(c):
                    last = act.activation(high, staged, ACT.Copy)
                last.then_inc(wh_done, 1)
                if c == 2:
                    act.wait_ge(const_done, 1)
                    for which in range(2):
                        qk_high(0, 0, which)
                    for t in range(NT):
                        v_high(0, t)
            work(0, tail=False, more=True)
            with act.Fori(1, NBLK - 1) as i:
                work(i, tail=True, more=True)
            work(NBLK - 1, tail=True, more=False)
            for s in range(9):
                tail_step(NBLK - 1, s)

        @block.vector
        def _(dve):
            def low(dst, src, bias, high, done):
                if bias is None:
                    dve.tensor_tensor(dst, src, high.bitcast(F32), ALU.subtract).then_inc(done, 1)
                else:
                    dve.scalar_tensor_tensor(out=dst, in0=src, scalar=bias, in1=high.bitcast(F32),
                                             op0=ALU.add, op1=ALU.subtract).then_inc(done, 1)

            def qk_low(i, p, which):
                n = i * PROJ + (which if p == 0 else QK0 + VP + 2 * (p - 1) + which)
                dve.wait_ge(proj_h, n + 1)
                low((ql, kl)[which][p % 2][0:PW, :], psum[0:PW, PROJ_BANK[which], :],
                    (nbq, bkc)[which][0:PW, p:p + 1], (qh, kh)[which][p % 2][0:PW, :], proj_l)

            def v_low(i, t):
                dve.wait_ge(proj_h, i * PROJ + QK0 + t + 1)
                low(v_l[:, t, :], psum[:, PROJ_BANK[t % 2], 0:D], None, v_h[:, t, :], proj_l)

            def maxima(i, s):
                dve.wait_ge(sc_done, i * STEPS + s + 1)
                since(dve, pt_done, i * STEPS + s - 2)
                if s == 0:
                    dve.wait_ge(nadj_done, i + 1)
                dve.sem_inc(dve_past, 1)
                b = s % BPB
                for q in range(QT):
                    c = s * QT + q
                    dve.tensor_tensor_reduce(prob[:, s % 3, q * N:(q + 1) * N],
                                             psum[:, SCORE_BANK[s % 2], q * N:(q + 1) * N],
                                             nadj[:, b * QT + q, :], 1.0, 3.0e38, ALU.add, ALU.min,
                                             nmax[:, c:c + 1]).then_inc(max_done, 1)

            def reciprocals(i, s):
                dve.wait_ge(exp_done, i * (STEPS * QT) + (s + 1) * QT)
                dve.reciprocal(rrec[:, s * QT:(s + 1) * QT], rsum[:, s * QT:(s + 1) * QT]).then_inc(rec_done, 1)

            def pt_low(i, s):
                dve.wait_ge(pt_hi, i * STEPS + s + 1)
                low(pt_l[:, s % 2, :], psum[:, PT_BANK[s % 2], :], None, pt_h[:, s % 2, :], pt_lo)

            def ctx_low(i, hd):
                p, a = hd // 2, hd % 2
                m = 64 if a == 0 else DH
                dve.wait_ge(ctx_hi, i * H + hd + 1)
                low(ctx_l[64 * a:64 * a + m, p, :], psum[0:m, CTX_BANK[hd % 2], :],
                    bvc[64 * a:64 * a + m, p:p + 1], ctx_h[64 * a:64 * a + m, p, :], ctx_lo)

            def residual1(i, t):
                dve.wait_ge(wo_done, i * NT + t + 1)
                dve.wait_ge(xb_done, i * NT + t + 1)
                since(dve, out_dma[t], i * 16)
                dve.tensor_tensor(x1[:, t, :], psum[:, WO_BANK[t], 0:D], xb[:, t, :], ALU.add).then_inc(t1_done, 1)

            def norm1(i, t):
                dve.wait_ge(r1_done, i * NT + t + 1)
                dve.scalar_tensor_tensor(out=x1[:, t, :], in0=x1[:, t, :], scalar=r1[:, t:t + 1], in1=a1_bc[:, :],
                                         op0=ALU.mult, op1=ALU.mult).then_inc(x1_done, 1)

            def x1t_low(i, k):
                dve.wait_ge(x1t_hi, i * KT + k + 1)
                low(x1t_l[:, k, :], psum[:, X1T_BANK[k], :], g1c[:, k:k + 1], x1t_h[:, k, :], x1t_lo)

            def hidden(i, f):
                dve.wait_ge(tz_done, i * FT + f + 1)
                dve.scalar_tensor_tensor(out=sil[:, f % 2, :], in0=tnh[:, f % 2, :], scalar=1.0, in1=sil[:, f % 2, :],
                                         op0=ALU.add, op1=ALU.mult).then_inc(g_done, 1)
                dve.wait_ge(g_hi, i * FT + f + 1)
                low(g_l[:, f % 4, :], sil[:, f % 2, :], None, g_h[:, f % 4, :], g_lo)

            def residual2(j, t):
                dve.wait_ge(f2_done, j * NT + t + 1)
                dve.wait_ge(x1b_done, j * NT + t + 1)
                dve.tensor_tensor(x1[:, t, :], psum[:, F2_BANK[t], 0:D], x1[:, t, :], ALU.add).then_inc(z_done, 1)

            def residual3(j, t):
                dve.wait_ge(za_done, j * NT + t + 1)
                dve.wait_ge(xg_done, j * NT + t + 1)
                dve.scalar_tensor_tensor(out=x1[:, t, :], in0=x1[:, t, :], scalar=r2[:, t:t + 1],
                                         in1=xg[:, t % 2, :], op0=ALU.mult, op1=ALU.add,
                                         accum_out=sw[:, t:t + 1]).then_inc(w_done, 1)

            def layer_norm(j, t):
                dve.wait_ge(rstd_done, j * NT + t + 1)
                dve.tensor_scalar(x1[:, t, :], x1[:, t, :], nmean[:, t:t + 1], rstd[:, t:t + 1],
                                  ALU.add, ALU.mult).then_inc(out_done, 1)

            def tail_step(j, s):
                if s == 0:
                    for t in range(NT):
                        residual2(j, t)
                if s in (2, 3, 5, 6):
                    residual3(j, {2: 0, 3: 1, 5: 2, 6: 3}[s])
                if s in (5, 6, 8, 9):
                    layer_norm(j, {5: 0, 6: 1, 8: 2, 9: 3}[s])

            def work(i, tail, more):
                for s in range(LAST + 1):
                    if tail and s == 0:
                        tail_step(i - 1, s)
                    if s < STEPS:
                        maxima(i, s)
                    p = s // 4 + 1
                    if p < NPAIR and s % 4 in (2, 3):
                        qk_low(i, p, s % 4 - 2)
                    if more and s in (17, 18):
                        qk_low(i + 1, 0, s - 17)
                    if s % 2 == 1 and 5 <= s <= LAST:
                        ctx_low(i, (s - 5) // 2)
                    if 1 <= s <= STEPS:
                        reciprocals(i, s - 1)
                    if 2 <= s < STEPS + 2:
                        pt_low(i, s - 2)
                    if tail and s > 0:
                        tail_step(i - 1, s)
                for t in range(NT):
                    residual1(i, t)
                if more:
                    v_low(i + 1, 0)
                norm1(i, 0)
                norm1(i, 1)
                if more:
                    v_low(i + 1, 1)
                norm1(i, 2)
                norm1(i, 3)
                if more:
                    v_low(i + 1, 2)
                for k in range(KT):
                    x1t_low(i, k)
                if more:
                    v_low(i + 1, NT - 1)
                for f in range(FT):
                    hidden(i, f)

            for w in (nbq, bkc, bvc):
                last = dve.memset(w[:, :], 0.0)
            for w in (wq_h, wq_l, wk_h, wk_l, wo_h, wo_l):
                last = dve.memset(w[:, :, :].bitcast(F32), 0.0)
            last.then_inc(zero_done, 1)
            for c in range(NCHUNK):
                dve.wait_ge(wh_done, c + 1)
                for staged, high, lo in chunk_parts(c):
                    last = dve.tensor_tensor(lo, staged, high.bitcast(F32), ALU.subtract)
                last.then_inc(wl_done, 1)
                if c == 2:
                    for which in range(2):
                        qk_low(0, 0, which)
                    for t in range(NT):
                        v_low(0, t)
            work(0, tail=False, more=True)
            with dve.Fori(1, NBLK - 1) as i:
                work(i, tail=True, more=True)
            work(NBLK - 1, tail=True, more=False)
            for s in range(10):
                tail_step(NBLK - 1, s)

        @block.tensor
        def _(pe):
            def three(o, ah, al, bh, bl, start=True, stop=True):
                pe.matmul(o, ah, bh, start=start, stop=False)
                pe.matmul(o, ah, bl, start=False, stop=False)
                return pe.matmul(o, al, bh, start=False, stop=stop)

            def qk_part(i, p, which, k):
                n = i * PROJ + (which if p == 0 else QK0 + VP + 2 * (p - 1) + which)
                if k == 0:
                    since(pe, proj_l, n - 1)
                if p == 0:
                    pe.wait_ge(xt_done, i * KT + k + 1)
                wh, wl = ((wq_h, wq_l), (wk_h, wk_l))[which]
                cols = slice(p * PW, (p + 1) * PW)
                last = three(psum[0:PW, PROJ_BANK[which], :], wh[:, k, cols], wl[:, k, cols],
                             xt_h[:, k, :], xt_l[:, k, :], start=(k == 0), stop=(k == KT - 1))
                if k == KT - 1:
                    last.then_inc(proj_done, 1)

            def v_tile(i, t):
                n = i * PROJ + QK0 + t
                since(pe, proj_l, n - 1)
                tok = slice(t * P, (t + 1) * P)
                for k in range(KT):
                    last = three(psum[:, PROJ_BANK[t % 2], 0:D], xt_h[:, k, tok], xt_l[:, k, tok],
                                 wv_h[:, k, :], wv_l[:, k, :], start=(k == 0), stop=(k == KT - 1))
                last.then_inc(proj_done, 1)

            def scores(i, s):
                p, a, b = s // 4, s // 2 % 2, s % 2
                if s % 4 == 0:
                    pe.wait_ge(proj_l, i * PROJ + (2 if p == 0 else QK0 + VP + 2 * p))
                if s >= 2:
                    pe.wait_ge(max_done, i * (STEPS * QT) + (s - 1) * QT)
                else:
                    since(pe, tz_done, i * FT)
                rows = slice(64 * a, 64 * a + DH)
                for q in range(QT):
                    qs = slice(b * N + q * P, b * N + (q + 1) * P)
                    ks = slice(b * N, (b + 1) * N)
                    last = three(psum[:, SCORE_BANK[s % 2], q * N:(q + 1) * N],
                                 qh[p % 2][rows, qs], ql[p % 2][rows, qs], kh[p % 2][rows, ks], kl[p % 2][rows, ks])
                last.then_inc(sc_done, 1)

            def transposes(i, s):
                pe.wait_ge(prob_done, i * STEPS + s + 1)
                if s >= 2:
                    pe.wait_ge(pt_lo, i * STEPS + s - 1)
                else:
                    since(pe, sq2_done, i * NT - NT + s + 1)
                for kt in range(QT):
                    for q in range(QT):
                        last = pe.transpose(psum[:, PT_BANK[s % 2], kt * N + q * P:kt * N + (q + 1) * P],
                                            prob[:, s % 3, q * N + kt * P:q * N + (kt + 1) * P], ident[:, :])
                last.then_inc(pt_done, 1)

            def context(i, s):
                hd, b = s // 2, s % 2
                m = 64 if hd % 2 == 0 else DH
                if s == 0:
                    pe.wait_ge(proj_l, i * PROJ + QK0 + VP)
                if b == 0:
                    if hd >= 2:
                        pe.wait_ge(ctx_lo, i * H + hd - 1)
                    else:
                        since(pe, sq2_done, i * NT - NT + 3 + hd)
                pe.wait_ge(pt_lo, i * STEPS + s + 1)
                cols = slice(hd * DH, hd * DH + m)
                for kt in range(QT):
                    ps = slice(kt * N, (kt + 1) * N)
                    last = three(psum[0:m, CTX_BANK[hd % 2], b * N:(b + 1) * N],
                                 v_h[:, b * QT + kt, cols], v_l[:, b * QT + kt, cols],
                                 pt_h[:, s % 2, ps], pt_l[:, s % 2, ps], start=(kt == 0), stop=(kt == QT - 1))
                last.then_inc(av_done, 1)

            def out_proj(i, t, pairs):
                if pairs[0] == 0:
                    if t < 2:
                        pe.wait_ge(max_done, i * (STEPS * QT) + (STEPS - 1 + t) * QT)
                    else:
                        pe.wait_ge(pt_lo, i * STEPS + STEPS - 3 + t)
                if t == 0:
                    pe.wait_ge(ctx_lo, i * H + 2 * (pairs[-1] + 1))
                tok = slice(t * P, (t + 1) * P)
                for p in pairs:
                    last = three(psum[:, WO_BANK[t], 0:D], ctx_h[0:PW, p, tok], ctx_l[0:PW, p, tok],
                                 wo_h[0:PW, p, :], wo_l[0:PW, p, :], start=(p == 0), stop=(p == NPAIR - 1))
                if pairs[-1] == NPAIR - 1:
                    last.then_inc(wo_done, 1)

            def x1_transposes(i):
                pe.wait_ge(x1_done, i * NT + NT)
                pe.wait_ge(ctx_lo, i * H + H)
                pe.wait_ge(sq1_done, i * NT + NT)
                for k in range(KT):
                    for t in range(NT):
                        last = pe.transpose(psum[:, X1T_BANK[k], t * P:(t + 1) * P],
                                            x1[:, t, k * P:(k + 1) * P], ident[:, :])
                    last.then_inc(x1t_done, 1)

            def ff1(i, f):
                if f == 0:
                    pe.wait_ge(x1t_lo, i * KT + KT)
                if f >= 2:
                    pe.wait_ge(tz_done, i * FT + f - 1)
                fs = slice(f * P, (f + 1) * P)
                for k in range(KT):
                    last = three(psum[:, F1_BANK[f % 2], :], w1_h[:, k, fs], w1_l[:, k, fs],
                                 x1t_h[:, k, :], x1t_l[:, k, :], start=(k == 0), stop=(k == KT - 1))
                last.then_inc(f1_done, 1)

            def ff2(i, f):
                pe.wait_ge(g_lo, i * FT + f + 1)
                for t in range(NT):
                    tok = slice(t * P, (t + 1) * P)
                    last = three(psum[:, F2_BANK[t], 0:D], g_h[:, f % 4, tok], g_l[:, f % 4, tok],
                                 w2_h[:, f, :], w2_l[:, f, :], start=(f == 0), stop=(f == FT - 1))
                    if f == FT - 1:
                        last.then_inc(f2_done, 1)
                if f < 8:
                    last.then_inc(f2_step, 1)

            def work(i, more):
                for s in range(STEPS + 3):
                    if s < STEPS:
                        scores(i, s)
                    if 2 <= s < STEPS + 2:
                        transposes(i, s - 2)
                    p = s // 4 + 1
                    if p < NPAIR and s % 4 < 3:
                        for n in (2 * (s % 4), 2 * (s % 4) + 1):
                            qk_part(i, p, n // KT, n % KT)
                    if more and s in (STEPS, STEPS + 1):
                        for k in range(KT):
                            qk_part(i + 1, 0, s - STEPS, k)
                    if s >= 3:
                        context(i, s - 3)
                for t in range(NT):
                    out_proj(i, t, (0, 1, 2))
                for t in range(NT):
                    out_proj(i, t, (3,))
                if more:
                    for t in range(NT - 1):
                        v_tile(i + 1, t)
                x1_transposes(i)
                if more:
                    v_tile(i + 1, NT - 1)
                for f in range(FT + 2):
                    if f < FT:
                        ff1(i, f)
                    if f >= 2:
                        ff2(i, f - 2)

            pe.wait_ge(ident_done, 2)
            pe.wait_ge(wl_done, 2)
            for which in range(2):
                for k in range(KT):
                    qk_part(0, 0, which, k)
            pe.wait_ge(wl_done, 3)
            for t in range(NT):
                v_tile(0, t)
            pe.wait_ge(wl_done, NCHUNK)
            work(0, more=True)
            with pe.Fori(1, NBLK - 1) as i:
                work(i, more=True)
            work(NBLK - 1, more=False)


_INS = ["x", "x_t", "adj"] + ["L0_gnn_" + n for n in (
    "wq", "bq", "wk", "bk", "wv", "bv", "wo", "bo", "w1", "b1", "w2", "b2", "alpha1", "gamma1", "alpha2", "gamma2")]


def kernel(**inputs):
    import numpy as _np
    import concourse.bacc as _bacc
    from concourse import mybir as _mybir
    from concourse.bass_utils import run_bass_kernel_spmd as _run

    nc = _bacc.Bacc("TRN2", target_bir_lowering=False, num_devices=1, dynamic_dma_scratch_size=1024)
    data = dict(inputs)
    x = _np.ascontiguousarray(inputs["x"])
    data["x_t"] = _np.ascontiguousarray(x.reshape(-1, x.shape[-1]).T)
    arrays, args = {}, []
    for name in _INS:
        a = _np.ascontiguousarray(data[name])
        arrays[f"in_{name}_dram"] = a
        args.append(nc.dram_tensor(f"in_{name}_dram", a.shape, _mybir.dt.from_np(a.dtype), kind="ExternalInput").ap())
    out = nc.dram_tensor("out_0_dram", x.shape, _mybir.dt.from_np(x.dtype), kind="ExternalOutput").ap()
    resnorm_kernel(nc, *args, out)
    r = _run(nc, [arrays], core_ids=[0])
    return r.results[0]["out_0_dram"]
```

```python
from contextlib import ExitStack

import concourse.bass as bass
from concourse import mybir

F32 = mybir.dt.float32
F32R = mybir.dt.float32r
ALU = mybir.AluOpType
ACT = mybir.ActivationFunctionType

P = 128
RMS_EPS = 1e-6
LN_EPS = 1e-5


def resnorm_kernel(nc, x, x_t, adj, wq, bq, wk, bk, wv, bv, wo, bo, w1, b1, w2, b2,
                   alpha1, gamma1, alpha2, gamma2, out):
    B, N, D = x.shape
    F = w1.shape[1]
    H = 8
    DH = D // H
    NPAIR = H // 2
    PW = 64 + DH
    KT = D // P
    FT = F // P
    BPB = 2
    TB = BPB * N
    NT = TB // P
    QT = N // P
    NBLK = B // BPB
    STEPS = H * BPB
    T_LAG, C_LAG = 3, 4
    LAST = STEPS + C_LAG
    TAIL = 14
    SLOTS = T_LAG + 1
    SCALE = float(DH) ** -0.5
    QK0, VP, QKP = 2, NT, 2 * (NPAIR - 1)
    PROJ = QK0 + VP + QKP
    PARTS = (3, 3, 1, 2, 1, 2, 1, 2, 1, 2, 1, 1, 1, 1, 1, 1)
    assert sum(PARTS) == NPAIR * 2 * KT
    assert N == 256 and D == 384 and B % BPB == 0 and PROJ % 2 == 0

    xf = x.rearrange("b n d -> (b n) d")
    outf = out.rearrange("b n d -> (b n) d")
    adj_v = adj.rearrange("b (t p) k -> p (b t) k", p=P)

    with ExitStack() as ctx:
        cursor = [nc.sbuf_base + (-nc.sbuf_base) % 64]

        def put(name, shape, dt=F32, at=None):
            size = 4
            for n in shape[1:]:
                size *= n
            if at is None:
                at = cursor[0]
                cursor[0] += size + (-size) % 32
            return nc.alloc_sbuf_tensor_at(name, shape, dt, offset=at)

        def sem(name):
            return ctx.enter_context(nc.semaphore(name))

        wq_h, wq_l, wk_h, wk_l = [put(n, [P, KT, NPAIR * PW], F32R) for n in ("wq_h", "wq_l", "wk_h", "wk_l")]
        wv_h, wv_l = put("wv_h", [P, KT, D], F32R), put("wv_l", [P, KT, D], F32R)
        wo_h, wo_l = put("wo_h", [P, NPAIR, D], F32R), put("wo_l", [P, NPAIR, D], F32R)
        w1_h, w1_l = put("w1_h", [P, KT, F], F32R), put("w1_l", [P, KT, F], F32R)
        w2_h, w2_l = put("w2_h", [P, FT, D], F32R), put("w2_l", [P, FT, D], F32R)
        bo_bc, gb2_bc, a1_bc, a2_bc, g2_bc = [
            put(n, [P, D]) for n in ("bo_bc", "gb2_bc", "a1_bc", "a2_bc", "g2_bc")]
        ident = put("ident", [P, P])
        nbq, bkc, bvc = put("nbq", [P, NPAIR]), put("bkc", [P, NPAIR]), put("bvc", [P, NPAIR])
        g1c, hb1 = put("g1c", [P, KT]), put("hb1", [P, FT])
        mhalf = put("mhalf", [P, 1])
        nmax, rsum, rrec = [put(n, [P, STEPS * QT]) for n in ("nmax", "rsum", "rrec")]
        ss1, ms1, r1 = [put(n, [P, NT]) for n in ("ss1", "ms1", "r1")]
        ss2, ms2, r2 = [put(n, [P, NT]) for n in ("ss2", "ms2", "r2")]
        sw, nmean, sv, msv, rstd = [put(n, [P, NT]) for n in ("sw", "nmean", "sv", "msv", "rstd")]
        v_h, v_l = put("v_h", [P, NT, D], F32R), put("v_l", [P, NT, D], F32R)
        nadj = put("nadj", [P, NT, N])
        xt_h, xt_l, xt_raw = [], [], []
        for n in range(2):
            xt_h.append(put(f"xt_h{n}", [P, KT, TB], F32R))
            xt_raw.append(put(f"xt_raw{n}", [P, KT, TB], at=cursor[0]))
            xt_l.append(put(f"xt_l{n}", [P, KT, TB], F32R))
        over_x1 = cursor[0]
        x1 = put("x1", [P, NT, D])
        xg = put("xg", [P, 2, D])
        junk = put("junk", [P, D])
        qh0, ql0, kh0, kl0 = [put(n, [P, TB], F32R) for n in ("qh0", "ql0", "kh0", "kl0")]
        over_ctx = cursor[0]
        ctx_h, ctx_l = put("ctx_h", [P, NPAIR, TB], F32R), put("ctx_l", [P, NPAIR, TB], F32R)
        g_h = put("g_h", [P, 4, TB], F32R, at=over_ctx)
        g_l = put("g_l", [P, 4, TB], F32R, at=over_ctx + 4 * TB * 4)
        over_att = cursor[0]
        qh1, ql1, kh1, kl1 = [put(n, [P, TB], F32R) for n in ("qh1", "ql1", "kh1", "kl1")]
        prob = put("prob", [P, SLOTS, QT * N])
        pt_h, pt_l = put("pt_h", [P, 2, TB], F32R), put("pt_l", [P, 2, TB], F32R)
        row = TB * 4
        x1t_h = put("x1t_h", [P, KT, TB], F32R, at=over_att)
        x1t_l = put("x1t_l", [P, KT, TB], F32R, at=over_att + KT * row)
        tnh = put("tnh", [P, 2, TB], at=over_att + 2 * KT * row)
        sil = put("sil", [P, 2, TB], at=over_att + (2 * KT + 2) * row)
        EARLY = 3
        LATE = 2 * D
        stage = [put(f"stage{n}", [P, KT * D], at=over_ctx + n * KT * D * 4) for n in range(EARLY)]
        stage += [put(f"stage_x1{n}", [P, LATE], at=over_x1 + n * LATE * 4) for n in range(2)]
        assert cursor[0] <= nc.sbuf_usable_end
        qh, ql, kh, kl = (qh0, qh1), (ql0, ql1), (kh0, kh1), (kl0, kl1)

        psum = ctx.enter_context(nc.psum_tensor("psum", [P, 8, 512], F32))
        PROJ_BANK, SCORE_BANK, PT_BANK, CTX_BANK = (0, 1), (2, 3), (4, 5), (6, 7)
        WO_BANK = (2, 3, 4, 5)
        X1T_BANK = (6, 7, 2)
        F1_BANK = (3, 2)
        F2_BANK = (4, 5, 6, 7)

        WO_CHUNKS, W1_CHUNKS, W2_CHUNKS = NPAIR // 2, KT * (F // LATE), FT // 2
        NCHUNK = EARLY + WO_CHUNKS + W1_CHUNKS + W2_CHUNKS
        w_in = [sem(f"w_in{n}") for n in range(NCHUNK)]
        const_in = sem("const_in")
        xt_in = [sem(f"xt_in{k}") for k in range(KT)]
        adj_in = sem("adj_in")
        x_in = [sem(f"x_in{t}") for t in range(NT)]
        xg_in = [sem(f"xg_in{t}") for t in range(2)]
        out_dma = [sem(f"out_dma{t}") for t in range(NT)]
        dve_past, pool_past = sem("dve_past"), sem("pool_past")
        zero_done = sem("zero_done")
        const_done = sem("const_done")
        ident_done = sem("ident_done")
        scaled = sem("scaled")
        wh_done = sem("wh_done")
        wl_done = sem("wl_done")
        proj_done = sem("proj_done")
        sc_done = sem("sc_done")
        pt_done = sem("pt_done")
        av_done = sem("av_done")
        wo_done = sem("wo_done")
        x1t_done = sem("x1t_done")
        f1_done = sem("f1_done")
        f2_step = sem("f2_step")
        f2_done = sem("f2_done")
        proj_h = sem("proj_h")
        pt_hi = sem("pt_hi")
        exp_done = sem("exp_done")
        ctx_hi = sem("ctx_hi")
        sq1_done = sem("sq1_done")
        x1t_hi = sem("x1t_hi")
        tz_done = sem("tz_done")
        g_hi = sem("g_hi")
        sq2_done = sem("sq2_done")
        var_done = sem("var_done")
        proj_l = sem("proj_l")
        max_done = sem("max_done")
        rec_done = sem("rec_done")
        pt_lo = sem("pt_lo")
        ctx_lo = sem("ctx_lo")
        t1_done = sem("t1_done")
        x1_done = sem("x1_done")
        x1t_lo = sem("x1t_lo")
        g_done = sem("g_done")
        g_lo = sem("g_lo")
        z_done = sem("z_done")
        w_done = sem("w_done")
        out_done = sem("out_done")
        prob_done = sem("prob_done")
        nadj_done = sem("nadj_done")
        xt_done = sem("xt_done")
        xt_hi = sem("xt_hi")
        x_done = sem("x_done")
        xg_done = sem("xg_done")
        ms1_done = sem("ms1_done")
        r1_done = sem("r1_done")
        x1b_done = sem("x1b_done")
        ms2_done = sem("ms2_done")
        r2_done = sem("r2_done")
        za_done = sem("za_done")
        nmean_done = sem("nmean_done")
        msv_done = sem("msv_done")
        rstd_done = sem("rstd_done")

        def since(eng, semaphore, count):
            if not (isinstance(count, int) and count <= 0):
                eng.wait_ge(semaphore, count)

        def parts_at(s):
            if s >= STEPS:
                return []
            n = sum(PARTS[:s])
            return [(1 + m // (2 * KT), m // KT % 2, m % KT) for m in range(n, n + PARTS[s])]

        def projected_before(s):
            return [(p, which) for p, which, k in parts_at(s - 1) if k == KT - 1] if s > 0 else []

        chunks = [("wq", 0), ("wk", 0), ("wv", 0)] + [("wo", n) for n in range(WO_CHUNKS)] \
            + [("w1", n) for n in range(W1_CHUNKS)] + [("w2", n) for n in range(W2_CHUNKS)]
        WO_WHOLE = EARLY + WO_CHUNKS
        W1_WHOLE = [WO_WHOLE + (k + 1) * (F // LATE) for k in range(KT)]
        W2_WHOLE = [W1_WHOLE[-1] + n + 1 for n in range(W2_CHUNKS)]

        def stage_of(c):
            return stage[c if c < EARLY else EARLY + (c - EARLY) % 2]

        def chunk_at(s):
            c = EARLY + s - 1
            return c if s >= 1 and c < NCHUNK else None

        def chunk_parts(c):
            name, n = chunks[c]
            s = stage_of(c)
            if name in ("wq", "wk"):
                h, l = (wq_h, wq_l) if name == "wq" else (wk_h, wk_l)
                parts = []
                for kk in range(KT):
                    for a in range(2):
                        src = s[:, kk * D:(kk + 1) * D].rearrange("p (r a d) -> p r a d", r=NPAIR, a=2)[:, :, a, :]
                        dst = [w[:, kk, :].rearrange("p (r c) -> p r c", r=NPAIR)[:, :, 64 * a:64 * a + DH]
                               for w in (h, l)]
                        parts.append((src, *dst))
                return parts
            if name == "wv":
                return [(s[:, 0:KT * D].rearrange("p (k n) -> p k n", k=KT), wv_h[:, :, :], wv_l[:, :, :])]
            if name == "wo":
                v = s[:, :].rearrange("p (r n) -> p r n", r=2)
                return [(v[64 * a:64 * a + DH], *[w[64 * a:64 * a + DH, 2 * n:2 * n + 2, :] for w in (wo_h, wo_l)])
                        for a in range(2)]
            if name == "w1":
                k, m = divmod(n * LATE, F)
                return [(s[:, :], w1_h[:, k, m:m + LATE], w1_l[:, k, m:m + LATE])]
            v = s[:, :].rearrange("p (g n) -> p g n", g=2)
            return [(v, w2_h[:, 2 * n:2 * n + 2, :], w2_l[:, 2 * n:2 * n + 2, :])]

        pair_biases = [(bq, nbq), (bk, bkc), (bv, bvc)]
        NCONST = 2 * len(pair_biases) + 2 + 6

        block = ctx.enter_context(nc.Block())

        @block.sync
        def _(sp):
            def load_chunk(c):
                name, n = chunks[c]
                s = stage_of(c)
                if c >= EARLY + 2:
                    sp.wait_ge(wl_done, c - 1)
                if name in ("wq", "wk", "wv"):
                    w = {"wq": wq, "wk": wk, "wv": wv}[name]
                    sp.dma_start(s[:, 0:KT * D].rearrange("p (k n) -> p k n", k=KT),
                                 w.rearrange("(k p) n -> p k n", p=P)).then_inc(w_in[c], 16)
                elif name == "wo":
                    v = s[:, :].rearrange("p (r n) -> p r n", r=2)
                    src = wo.rearrange("(r a d) n -> a d r n", r=NPAIR, a=2)
                    for a in range(2):
                        sp.dma_start(v[64 * a:64 * a + DH], src[a, :, 2 * n:2 * n + 2, :]).then_inc(w_in[c], 16)
                elif name == "w1":
                    k, m = divmod(n * LATE, F)
                    sp.dma_start(s[:, :], w1[k * P:(k + 1) * P, m:m + LATE]).then_inc(w_in[c], 16)
                else:
                    sp.dma_start(s[:, :].rearrange("p (g n) -> p g n", g=2),
                                 w2[2 * n * P:2 * (n + 1) * P, :].rearrange("(g p) n -> p g n", p=P)
                                 ).then_inc(w_in[c], 16)

            def load_xt(i, odd, k):
                sp.dma_start(xt_raw[odd][:, k, :], x_t[k * P:(k + 1) * P, bass.ds(i * TB, TB)])\
                    .then_inc(xt_in[k], 16)

            def load_adj(i):
                sp.dma_start(nadj[:, :, :], adj_v[:, bass.ds(i * NT, NT), :]).then_inc(adj_in, 16)

            def load_x(dst, i, t, arrived):
                sp.dma_start(dst, xf[bass.ds(i * TB + t * P, P), :]).then_inc(arrived, 16)

            def loads_and_stores(i, odd, tail=True, more=True):
                if more:
                    since(sp, proj_done, i * PROJ)
                    for k in range(KT):
                        sp.wait_ge(xt_done, i * KT + k + 1)
                        load_xt(i + 1, 1 - odd, k)
                if tail:
                    j = i - 1
                    for t in range(2):
                        sp.wait_ge(w_done, j * NT + t + 1)
                        load_x(xg[:, t, :], j, t + 2, xg_in[t])
                    for t in range(NT):
                        sp.wait_ge(out_done, j * NT + t + 1)
                        sp.dma_start(outf[bass.ds(j * TB + t * P, P), :], x1[:, t, :]).then_inc(out_dma[t], 16)
                else:
                    for c in range(EARLY, NCHUNK):
                        load_chunk(c)
                    sp.wait_ge(wl_done, NCHUNK)
                for t in range(NT):
                    since(sp, out_dma[t], i * 16)
                    load_x(x1[:, t, :], i, t, x_in[t])
                if more:
                    sp.wait_ge(max_done, i * (STEPS * QT) + STEPS * QT)
                    load_adj(i + 1)
                for t in range(2):
                    since(sp, w_done, i * NT - NT + t + 3)
                    load_x(xg[:, t, :], i, t, xg_in[t])

            load_chunk(0)
            for k in range(KT):
                load_xt(0, 0, k)
            load_chunk(1)
            load_chunk(2)
            sp.wait_ge(zero_done, 1)
            for dram, tile in pair_biases:
                src = dram.rearrange("(r a d) -> a d r", r=NPAIR, a=2)
                for a in range(2):
                    sp.dma_start(tile[64 * a:64 * a + DH, :], src[a], allow_slow_non_contiguous=True).then_inc(const_in, 16)
            sp.dma_start(g1c[:, :], gamma1.rearrange("(k p) -> p k", p=P), allow_slow_non_contiguous=True).then_inc(const_in, 16)
            sp.dma_start(hb1[:, :], b1.rearrange("(f p) -> p f", p=P), allow_slow_non_contiguous=True).then_inc(const_in, 16)
            for tile, dram in ((bo_bc, bo), (gb2_bc, gamma1), (a1_bc, alpha1), (a2_bc, alpha2),
                               (g2_bc, gamma2), (junk, b2)):
                sp.dma_start(tile[:, :], dram.partition_broadcast(P)).then_inc(const_in, 16)
            load_adj(0)

            loads_and_stores(0, 0, tail=False)
            with sp.Fori(1, NBLK - 2, 2) as i:
                loads_and_stores(i, 1)
                loads_and_stores(i + 1, 0)
            loads_and_stores(NBLK - 1, 1, more=False)
            j = NBLK - 1
            for t in range(2):
                sp.wait_ge(w_done, j * NT + t + 1)
                load_x(xg[:, t, :], j, t + 2, xg_in[t])
            for t in range(NT):
                sp.wait_ge(out_done, j * NT + t + 1)
                sp.dma_start(outf[j * TB + t * P:j * TB + (t + 1) * P, :], x1[:, t, :]).then_inc(out_dma[t], 16)
            for t in range(NT):
                sp.wait_ge(out_dma[t], 16 * NBLK)

        @block.gpsimd
        def _(pool):
            def split_xt(i, odd, k):
                pool.wait_ge(xt_in[k], i * 16 + 16)
                pool.sem_inc(pool_past, 1)
                raw, high, low = xt_raw[odd][:, k, :], xt_h[odd][:, k, :], xt_l[odd][:, k, :]
                pool.tensor_scalar(high, raw, 1.0, 0.0, ALU.mult, ALU.add).then_inc(xt_hi, 1)
                pool.wait_ge(xt_hi, i * KT + k + 1)
                pool.tensor_tensor(low, raw, high.bitcast(F32), ALU.subtract).then_inc(xt_done, 1)

            def negate_adj(i):
                pool.wait_ge(adj_in, i * 16 + 16)
                pool.sem_inc(pool_past, 1)
                pool.tensor_scalar(nadj[:, :, :], nadj[:, :, :], -1.0, 0.0, ALU.mult, ALU.add).then_inc(nadj_done, 1)

            def normalise(i, s):
                pool.wait_ge(rec_done, i * STEPS + s + 1)
                pool.sem_inc(pool_past, 1)
                for q in range(QT):
                    c = s * QT + q
                    last = pool.tensor_scalar(prob[:, s % SLOTS, q * N:(q + 1) * N], prob[:, s % SLOTS, q * N:(q + 1) * N],
                                              rrec[:, c:c + 1], 0.0, ALU.mult, ALU.add)
                last.then_inc(prob_done, 1)

            def add_bo(i, t):
                pool.wait_ge(x_in[t], i * 16 + 16)
                pool.tensor_tensor(x1[:, t, :], x1[:, t, :], bo_bc[:, :], ALU.add).then_inc(x_done, 1)

            def add_xg(j, t):
                pool.wait_ge(xg_in[t % 2], j * 32 + 16 * (t // 2) + 16)
                pool.tensor_tensor(xg[:, t % 2, :], xg[:, t % 2, :], g2_bc[:, :], ALU.add).then_inc(xg_done, 1)

            def rsqrt_mean(sums, mean, root, t, eps, mean_done, root_done, count):
                pool.sem_inc(pool_past, 1)
                pool.tensor_scalar(mean[:, t:t + 1], sums[:, t:t + 1], 1.0 / D, eps, ALU.mult, ALU.add)\
                    .then_inc(mean_done, 1)
                pool.wait_ge(mean_done, count)
                pool.tensor_tensor(root[:, t:t + 1], mean[:, t:t + 1], mhalf[:, 0:1], ALU.pow).then_inc(root_done, 1)

            def norm1_root(i, t):
                pool.wait_ge(sq1_done, i * NT + t + 1)
                rsqrt_mean(ss1, ms1, r1, t, RMS_EPS, ms1_done, r1_done, i * NT + t + 1)

            def add_b2(i, t):
                pool.wait_ge(x1t_done, i * KT + KT)
                pool.tensor_tensor(x1[:, t, :], x1[:, t, :], gb2_bc[:, :], ALU.add).then_inc(x1b_done, 1)

            def norm2_root(j, t):
                pool.wait_ge(sq2_done, j * NT + t + 1)
                rsqrt_mean(ss2, ms2, r2, t, RMS_EPS, ms2_done, r2_done, j * NT + t + 1)

            def layer_mean(j, t):
                pool.wait_ge(w_done, j * NT + t + 1)
                pool.sem_inc(pool_past, 1)
                pool.tensor_scalar(nmean[:, t:t + 1], sw[:, t:t + 1], -1.0 / D, 0.0, ALU.mult, ALU.add)\
                    .then_inc(nmean_done, 1)

            def layer_root(j, t):
                pool.wait_ge(var_done, j * NT + t + 1)
                rsqrt_mean(sv, msv, rstd, t, LN_EPS, msv_done, rstd_done, j * NT + t + 1)

            def tail_step(j, s):
                if s == 0:
                    for t in range(NT):
                        norm2_root(j, t)
                for t in range(NT):
                    if s == (2, 3, 6, 7)[t]:
                        layer_mean(j, t)
                    if s == (5, 6, 9, 10)[t]:
                        layer_root(j, t)
                if s in (4, 5):
                    add_xg(j, s - 2)

            def work(i, odd, tail=True, more=True):
                for s in range(STEPS):
                    if tail:
                        tail_step(i - 1, s)
                    normalise(i, s)
                    if more and s in (6, 8, 9):
                        split_xt(i + 1, 1 - odd, (6, 8, 9).index(s))
                for t in range(NT):
                    add_bo(i, t)
                for t in range(NT):
                    norm1_root(i, t)
                for t in range(NT):
                    add_b2(i, t)
                if more:
                    negate_adj(i + 1)
                for t in range(2):
                    add_xg(i, t)

            pool.memset(ident[:, :], 0.0).then_inc(ident_done, 1)
            pool.memset(mhalf[:, :], -0.5)
            pool.wait_ge(ident_done, 1)
            pool.affine_select(out=ident[:, :], in_=ident[:, :], compare_op=ALU.not_equal, fill=1.0, base=0,
                               pattern=[[-1, P]], channel_multiplier=1).then_inc(ident_done, 1)
            pool.wait_ge(w_in[0], 16)
            pool.tensor_scalar(stage[0][:, 0:KT * D], stage[0][:, 0:KT * D], -SCALE, 0.0, ALU.mult, ALU.add)\
                .then_inc(scaled, 1)
            for k in range(KT):
                split_xt(0, 0, k)
            pool.wait_ge(const_in, 16 * NCONST)
            pool.tensor_scalar(nbq[:, :], nbq[:, :], -SCALE, 0.0, ALU.mult, ALU.add)
            pool.tensor_scalar(hb1[:, :], hb1[:, :], 0.5, 0.0, ALU.mult, ALU.add)
            pool.tensor_tensor(gb2_bc[:, :], gb2_bc[:, :], junk[:, :], ALU.add).then_inc(const_done, 1)
            negate_adj(0)

            work(0, 0, tail=False)
            with pool.Fori(1, NBLK - 2, 2) as i:
                work(i, 1)
                work(i + 1, 0)
            work(NBLK - 1, 1, more=False)
            for s in range(TAIL):
                tail_step(NBLK - 1, s)

        @block.scalar
        def _(act):
            def weights_high(c):
                act.wait_ge(w_in[c], 32 if chunks[c][0] == "wo" else 16)
                if c == 0:
                    act.wait_ge(scaled, 1)
                for staged, high, _ in chunk_parts(c):
                    last = act.activation(high, staged, ACT.Copy)
                last.then_inc(wh_done, 1)

            def proj_high(n, bank, dst, bias=None):
                act.wait_ge(proj_done, n + 1)
                src = psum[0:dst.shape[0], bank, 0:dst.shape[1]]
                if bias is None:
                    act.activation(dst, src, ACT.Copy).then_inc(proj_h, 1)
                else:
                    act.activation(dst, src, ACT.Identity, bias=bias).then_inc(proj_h, 1)

            def qk_high(i, p, which):
                n = i * PROJ + (which if p == 0 else QK0 + VP + 2 * (p - 1) + which)
                since(act, sc_done, i * STEPS + 4 * (p - 1))
                proj_high(n, PROJ_BANK[which], (qh, kh)[which][p % 2][0:PW, :], (nbq, bkc)[which][0:PW, p:p + 1])

            def v_high(i, t):
                since(act, av_done, i * STEPS)
                proj_high(i * PROJ + QK0 + t, PROJ_BANK[t % 2], v_h[:, t, :])

            def exponentials(i, s):
                for q in range(QT):
                    c = s * QT + q
                    act.wait_ge(max_done, i * (STEPS * QT) + c + 1)
                    part = prob[:, s % SLOTS, q * N:(q + 1) * N]
                    act.activation(part, part, ACT.Exp, bias=nmax[:, c:c + 1], scale=-1.0,
                                   accum_out=rsum[:, c:c + 1]).then_inc(exp_done, 1)

            def pt_high(i, s):
                act.wait_ge(pt_done, i * STEPS + s + 1)
                since(act, av_done, i * STEPS + s - 1)
                act.activation(pt_h[:, s % 2, :], psum[:, PT_BANK[s % 2], :], ACT.Copy).then_inc(pt_hi, 1)

            def ctx_high(i, hd):
                p, a = hd // 2, hd % 2
                m = 64 if a == 0 else DH
                act.wait_ge(av_done, i * STEPS + 2 * hd + 2)
                act.activation(ctx_h[64 * a:64 * a + m, p, :], psum[0:m, CTX_BANK[hd % 2], :], ACT.Identity,
                               bias=bvc[64 * a:64 * a + m, p:p + 1]).then_inc(ctx_hi, 1)

            def square1(i, t):
                act.wait_ge(t1_done, i * NT + t + 1)
                act.activation(psum[:, WO_BANK[t], 0:D], x1[:, t, :], ACT.Square,
                               accum_out=ss1[:, t:t + 1]).then_inc(sq1_done, 1)

            def x1t_high(i, k):
                act.wait_ge(x1t_done, i * KT + k + 1)
                act.activation(x1t_h[:, k, :], psum[:, X1T_BANK[k], :], ACT.Identity,
                               bias=g1c[:, k:k + 1]).then_inc(x1t_hi, 1)

            def silu_terms(i, f):
                act.wait_ge(f1_done, i * FT + f + 1)
                if f >= 2:
                    act.wait_ge(g_lo, i * FT + f - 1)
                src = psum[:, F1_BANK[f % 2], :]
                act.activation(tnh[:, f % 2, :], src, ACT.Tanh, bias=hb1[:, f:f + 1], scale=0.5)
                act.activation(sil[:, f % 2, :], src, ACT.Identity, bias=hb1[:, f:f + 1], scale=0.5)\
                    .then_inc(tz_done, 1)

            def hidden_high(i, f):
                act.wait_ge(g_done, i * FT + f + 1)
                if f >= 4:
                    act.wait_ge(f2_step, i * 8 + f - 3)
                act.activation(g_h[:, f % 4, :], sil[:, f % 2, :], ACT.Copy).then_inc(g_hi, 1)

            def square2(j, t):
                act.wait_ge(z_done, j * NT + t + 1)
                act.activation(psum[:, F2_BANK[t], 0:D], x1[:, t, :], ACT.Square,
                               accum_out=ss2[:, t:t + 1]).then_inc(sq2_done, 1)

            def variance(j, t):
                act.wait_ge(nmean_done, j * NT + t + 1)
                since(act, var_done, j * NT + t)
                act.activation(junk[:, :], x1[:, t, :], ACT.Square, bias=nmean[:, t:t + 1],
                               accum_out=sv[:, t:t + 1]).then_inc(var_done, 1)

            def tail_step(j, s):
                if s == 0:
                    for t in range(NT):
                        square2(j, t)
                for t in range(NT):
                    if s == (6, 7, 10, 11)[t]:
                        variance(j, t)

            def work(i, odd, tail=True, more=True):
                for s in range(LAST + 1):
                    if tail:
                        tail_step(i - 1, s)
                    for p, which in projected_before(s):
                        if p < NPAIR:
                            qk_high(i, p, which)
                        elif more:
                            qk_high(i + 1, 0, which)
                    if s >= C_LAG + 2 and (s - C_LAG) % 2 == 0:
                        ctx_high(i, (s - C_LAG - 2) // 2)
                    if T_LAG <= s < STEPS + T_LAG:
                        pt_high(i, s - T_LAG)
                    if s < STEPS:
                        exponentials(i, s)
                    if not tail and chunk_at(s) is not None:
                        weights_high(chunk_at(s))
                if more:
                    for t in range(2):
                        v_high(i + 1, t)
                for t in range(NT):
                    square1(i, t)
                for k in range(KT):
                    x1t_high(i, k)
                if more:
                    for t in range(2, NT):
                        v_high(i + 1, t)
                for f in range(FT):
                    silu_terms(i, f)
                    hidden_high(i, f)

            act.wait_ge(zero_done, 1)
            for c in range(EARLY):
                weights_high(c)
            act.wait_ge(const_done, 1)
            for which in range(2):
                qk_high(0, 0, which)
            for t in range(NT):
                v_high(0, t)
            work(0, 0, tail=False)
            with act.Fori(1, NBLK - 2, 2) as i:
                work(i, 1)
                work(i + 1, 0)
            work(NBLK - 1, 1, more=False)
            for s in range(TAIL):
                tail_step(NBLK - 1, s)

        @block.vector
        def _(dve):
            def low(dst, src, bias, high, done):
                if bias is None:
                    dve.tensor_tensor(dst, src, high.bitcast(F32), ALU.subtract).then_inc(done, 1)
                else:
                    dve.scalar_tensor_tensor(out=dst, in0=src, scalar=bias, in1=high.bitcast(F32),
                                             op0=ALU.add, op1=ALU.subtract).then_inc(done, 1)

            def weights_low(c):
                dve.wait_ge(wh_done, c + 1)
                for staged, high, lo in chunk_parts(c):
                    last = dve.tensor_tensor(lo, staged, high.bitcast(F32), ALU.subtract)
                last.then_inc(wl_done, 1)

            def qk_low(i, p, which):
                n = i * PROJ + (which if p == 0 else QK0 + VP + 2 * (p - 1) + which)
                dve.wait_ge(proj_h, n + 1)
                low((ql, kl)[which][p % 2][0:PW, :], psum[0:PW, PROJ_BANK[which], :],
                    (nbq, bkc)[which][0:PW, p:p + 1], (qh, kh)[which][p % 2][0:PW, :], proj_l)

            def v_low(i, t):
                dve.wait_ge(proj_h, i * PROJ + QK0 + t + 1)
                low(v_l[:, t, :], psum[:, PROJ_BANK[t % 2], 0:D], None, v_h[:, t, :], proj_l)

            def maxima(i, s):
                dve.wait_ge(sc_done, i * STEPS + s + 1)
                since(dve, pt_done, i * STEPS + s - SLOTS + 1)
                if s == 0:
                    dve.wait_ge(nadj_done, i + 1)
                dve.sem_inc(dve_past, 1)
                b = s % BPB
                for q in range(QT):
                    c = s * QT + q
                    dve.tensor_tensor_reduce(prob[:, s % SLOTS, q * N:(q + 1) * N],
                                             psum[:, SCORE_BANK[s % 2], q * N:(q + 1) * N],
                                             nadj[:, b * QT + q, :], 1.0, 3.0e38, ALU.add, ALU.min,
                                             nmax[:, c:c + 1]).then_inc(max_done, 1)

            def reciprocals(i, s):
                dve.wait_ge(exp_done, i * (STEPS * QT) + (s + 1) * QT)
                dve.reciprocal(rrec[:, s * QT:(s + 1) * QT], rsum[:, s * QT:(s + 1) * QT]).then_inc(rec_done, 1)

            def pt_low(i, s):
                dve.wait_ge(pt_hi, i * STEPS + s + 1)
                low(pt_l[:, s % 2, :], psum[:, PT_BANK[s % 2], :], None, pt_h[:, s % 2, :], pt_lo)

            def ctx_low(i, hd):
                p, a = hd // 2, hd % 2
                m = 64 if a == 0 else DH
                dve.wait_ge(ctx_hi, i * H + hd + 1)
                low(ctx_l[64 * a:64 * a + m, p, :], psum[0:m, CTX_BANK[hd % 2], :],
                    bvc[64 * a:64 * a + m, p:p + 1], ctx_h[64 * a:64 * a + m, p, :], ctx_lo)

            def residual1(i, t):
                dve.wait_ge(wo_done, i * NT + t + 1)
                dve.wait_ge(x_done, i * NT + t + 1)
                dve.tensor_tensor(x1[:, t, :], psum[:, WO_BANK[t], 0:D], x1[:, t, :], ALU.add).then_inc(t1_done, 1)

            def norm1(i, t):
                dve.wait_ge(r1_done, i * NT + t + 1)
                dve.scalar_tensor_tensor(out=x1[:, t, :], in0=x1[:, t, :], scalar=r1[:, t:t + 1], in1=a1_bc[:, :],
                                         op0=ALU.mult, op1=ALU.mult).then_inc(x1_done, 1)

            def x1t_low(i, k):
                dve.wait_ge(x1t_hi, i * KT + k + 1)
                low(x1t_l[:, k, :], psum[:, X1T_BANK[k], :], g1c[:, k:k + 1], x1t_h[:, k, :], x1t_lo)

            def hidden(i, f):
                dve.wait_ge(tz_done, i * FT + f + 1)
                dve.scalar_tensor_tensor(out=sil[:, f % 2, :], in0=tnh[:, f % 2, :], scalar=1.0, in1=sil[:, f % 2, :],
                                         op0=ALU.add, op1=ALU.mult).then_inc(g_done, 1)
                dve.wait_ge(g_hi, i * FT + f + 1)
                low(g_l[:, f % 4, :], sil[:, f % 2, :], None, g_h[:, f % 4, :], g_lo)

            def residual2(j, t):
                dve.wait_ge(f2_done, j * NT + t + 1)
                dve.wait_ge(x1b_done, j * NT + t + 1)
                dve.tensor_tensor(x1[:, t, :], psum[:, F2_BANK[t], 0:D], x1[:, t, :], ALU.add).then_inc(z_done, 1)

            def times_alpha2(j, t):
                dve.wait_ge(sq2_done, j * NT + t + 1)
                dve.tensor_tensor(x1[:, t, :], x1[:, t, :], a2_bc[:, :], ALU.mult).then_inc(za_done, 1)

            def residual3(j, t):
                dve.wait_ge(za_done, j * NT + t + 1)
                dve.wait_ge(r2_done, j * NT + t + 1)
                dve.wait_ge(xg_done, j * NT + t + 1)
                dve.scalar_tensor_tensor(out=x1[:, t, :], in0=x1[:, t, :], scalar=r2[:, t:t + 1],
                                         in1=xg[:, t % 2, :], op0=ALU.mult, op1=ALU.add,
                                         accum_out=sw[:, t:t + 1]).then_inc(w_done, 1)

            def layer_norm(j, t):
                dve.wait_ge(rstd_done, j * NT + t + 1)
                dve.tensor_scalar(x1[:, t, :], x1[:, t, :], nmean[:, t:t + 1], rstd[:, t:t + 1],
                                  ALU.add, ALU.mult).then_inc(out_done, 1)

            def tail_step(j, s):
                if s in (1, 2):
                    times_alpha2(j, 2 * s - 2)
                    times_alpha2(j, 2 * s - 1)
                for t in range(NT):
                    if s == (3, 4, 7, 8)[t]:
                        residual3(j, t)
                    if s == (8, 9, 12, 13)[t]:
                        layer_norm(j, t)

            def work(i, odd, tail=True, more=True):
                for s in range(LAST + 1):
                    if tail and s == 0:
                        residual2(i - 1, 0)
                        residual2(i - 1, 1)
                    if s < STEPS:
                        maxima(i, s)
                    if tail and s == 0:
                        residual2(i - 1, 2)
                        residual2(i - 1, 3)
                    for p, which in projected_before(s):
                        if p < NPAIR:
                            qk_low(i, p, which)
                        elif more:
                            qk_low(i + 1, 0, which)
                    if s >= C_LAG + 2 and (s - C_LAG) % 2 == 0:
                        ctx_low(i, (s - C_LAG - 2) // 2)
                    if 1 <= s <= STEPS:
                        reciprocals(i, s - 1)
                    if T_LAG <= s < STEPS + T_LAG:
                        pt_low(i, s - T_LAG)
                    if tail and s > 0:
                        tail_step(i - 1, s)
                    if not tail and chunk_at(s) is not None:
                        weights_low(chunk_at(s))
                if more:
                    for t in range(2):
                        v_low(i + 1, t)
                for t in range(NT):
                    residual1(i, t)
                    if t > 0:
                        norm1(i, t - 1)
                norm1(i, NT - 1)
                for k in range(KT):
                    x1t_low(i, k)
                if more:
                    for t in range(2, NT):
                        v_low(i + 1, t)
                for f in range(FT):
                    hidden(i, f)

            for w in (nbq, bkc, bvc):
                last = dve.memset(w[:, :], 0.0)
            for w in (wq_h, wq_l, wk_h, wk_l):
                gaps = w[:, :, :].rearrange("p k (r c) -> p (k r) c", r=NPAIR)[:, :, DH:64]
                last = dve.memset(gaps.bitcast(F32), 0.0)
            for w in (wo_h, wo_l):
                last = dve.memset(w[32:64, :, :].bitcast(F32), 0.0)
            last.then_inc(zero_done, 1)
            for c in range(EARLY):
                weights_low(c)
            for which in range(2):
                qk_low(0, 0, which)
            for t in range(NT):
                v_low(0, t)
            work(0, 0, tail=False)
            with dve.Fori(1, NBLK - 2, 2) as i:
                work(i, 1)
                work(i + 1, 0)
            work(NBLK - 1, 1, more=False)
            for t in range(NT):
                residual2(NBLK - 1, t)
            for s in range(1, TAIL):
                tail_step(NBLK - 1, s)

        @block.tensor
        def _(pe):
            def three(o, ah, al, bh, bl, start=True, stop=True):
                pe.matmul(o, ah, bh, start=start, stop=False)
                pe.matmul(o, ah, bl, start=False, stop=False)
                return pe.matmul(o, al, bh, start=False, stop=stop)

            def qk_part(i, odd, p, which, k):
                n = i * PROJ + (which if p == 0 else QK0 + VP + 2 * (p - 1) + which)
                if k == 0:
                    since(pe, proj_l, n - 1)
                if p == 0:
                    pe.wait_ge(xt_done, i * KT + k + 1)
                wh, wl = ((wq_h, wq_l), (wk_h, wk_l))[which]
                cols = slice(p * PW, (p + 1) * PW)
                last = three(psum[0:PW, PROJ_BANK[which], :], wh[:, k, cols], wl[:, k, cols],
                             xt_h[odd][:, k, :], xt_l[odd][:, k, :], start=(k == 0), stop=(k == KT - 1))
                if k == KT - 1:
                    last.then_inc(proj_done, 1)

            def v_tile(i, odd, t):
                n = i * PROJ + QK0 + t
                since(pe, proj_l, n - 1)
                tok = slice(t * P, (t + 1) * P)
                for k in range(KT):
                    last = three(psum[:, PROJ_BANK[t % 2], 0:D], xt_h[odd][:, k, tok], xt_l[odd][:, k, tok],
                                 wv_h[:, k, :], wv_l[:, k, :], start=(k == 0), stop=(k == KT - 1))
                last.then_inc(proj_done, 1)

            def scores(i, s):
                p, a, b = s // 4, s // 2 % 2, s % 2
                if s % 4 == 0:
                    pe.wait_ge(proj_l, i * PROJ + (2 if p == 0 else QK0 + VP + 2 * p))
                if s >= 2:
                    pe.wait_ge(max_done, i * (STEPS * QT) + (s - 1) * QT)
                else:
                    since(pe, tz_done, i * FT)
                rows = slice(64 * a, 64 * a + DH)
                for q in range(QT):
                    qs = slice(b * N + q * P, b * N + (q + 1) * P)
                    ks = slice(b * N, (b + 1) * N)
                    last = three(psum[:, SCORE_BANK[s % 2], q * N:(q + 1) * N],
                                 qh[p % 2][rows, qs], ql[p % 2][rows, qs], kh[p % 2][rows, ks], kl[p % 2][rows, ks])
                last.then_inc(sc_done, 1)

            def transposes(i, s):
                pe.wait_ge(prob_done, i * STEPS + s + 1)
                if s >= 2:
                    pe.wait_ge(pt_lo, i * STEPS + s - 1)
                else:
                    since(pe, sq2_done, i * NT - NT + s + 1)
                for kt in range(QT):
                    for q in range(QT):
                        last = pe.transpose(psum[:, PT_BANK[s % 2], kt * N + q * P:kt * N + (q + 1) * P],
                                            prob[:, s % SLOTS, q * N + kt * P:q * N + (kt + 1) * P], ident[:, :])
                last.then_inc(pt_done, 1)

            def context(i, s):
                hd, b = s // 2, s % 2
                m = 64 if hd % 2 == 0 else DH
                if s == 0:
                    pe.wait_ge(proj_l, i * PROJ + QK0 + VP)
                if b == 0:
                    if hd >= 2:
                        pe.wait_ge(ctx_lo, i * H + hd - 1)
                    else:
                        since(pe, sq2_done, i * NT - NT + 3 + hd)
                pe.wait_ge(pt_lo, i * STEPS + s + 1)
                cols = slice(hd * DH, hd * DH + m)
                for kt in range(QT):
                    ps = slice(kt * N, (kt + 1) * N)
                    last = three(psum[0:m, CTX_BANK[hd % 2], b * N:(b + 1) * N],
                                 v_h[:, b * QT + kt, cols], v_l[:, b * QT + kt, cols],
                                 pt_h[:, s % 2, ps], pt_l[:, s % 2, ps], start=(kt == 0), stop=(kt == QT - 1))
                last.then_inc(av_done, 1)

            def out_proj(i, t):
                if t < 2:
                    pe.wait_ge(max_done, i * (STEPS * QT) + (STEPS - 1 + t) * QT)
                else:
                    pe.wait_ge(pt_lo, i * STEPS + STEPS - 3 + t)
                tok = slice(t * P, (t + 1) * P)
                for p in range(NPAIR):
                    if t == 0:
                        pe.wait_ge(ctx_lo, i * H + 2 * (p + 1))
                        pe.wait_ge(wl_done, WO_WHOLE)
                    last = three(psum[:, WO_BANK[t], 0:D], ctx_h[0:PW, p, tok], ctx_l[0:PW, p, tok],
                                 wo_h[0:PW, p, :], wo_l[0:PW, p, :], start=(p == 0), stop=(p == NPAIR - 1))
                last.then_inc(wo_done, 1)

            def x1_transposes(i, t):
                pe.wait_ge(x1_done, i * NT + t + 1)
                if t == 0:
                    pe.wait_ge(sq1_done, i * NT + 1)
                for k in range(KT):
                    last = pe.transpose(psum[:, X1T_BANK[k], t * P:(t + 1) * P],
                                        x1[:, t, k * P:(k + 1) * P], ident[:, :])
                    if t == NT - 1:
                        last.then_inc(x1t_done, 1)

            def ff1(i, f):
                if f == 0:
                    pe.wait_ge(sq1_done, i * NT + 2)
                if f >= 2:
                    pe.wait_ge(tz_done, i * FT + f - 1)
                fs = slice(f * P, (f + 1) * P)
                for k in range(KT):
                    if f == 0:
                        pe.wait_ge(x1t_lo, i * KT + k + 1)
                        pe.wait_ge(wl_done, W1_WHOLE[k])
                    last = three(psum[:, F1_BANK[f % 2], :], w1_h[:, k, fs], w1_l[:, k, fs],
                                 x1t_h[:, k, :], x1t_l[:, k, :], start=(k == 0), stop=(k == KT - 1))
                last.then_inc(f1_done, 1)

            def ff2(i, f):
                pe.wait_ge(g_lo, i * FT + f + 1)
                if f % 2 == 0:
                    pe.wait_ge(wl_done, W2_WHOLE[f // 2])
                for t in range(NT):
                    tok = slice(t * P, (t + 1) * P)
                    last = three(psum[:, F2_BANK[t], 0:D], g_h[:, f % 4, tok], g_l[:, f % 4, tok],
                                 w2_h[:, f, :], w2_l[:, f, :], start=(f == 0), stop=(f == FT - 1))
                    if f == FT - 1:
                        last.then_inc(f2_done, 1)
                if f < 8:
                    last.then_inc(f2_step, 1)

            def work(i, odd, more=True):
                for s in range(STEPS + C_LAG):
                    if s < STEPS:
                        scores(i, s)
                    if T_LAG <= s < STEPS + T_LAG:
                        transposes(i, s - T_LAG)
                    for p, which, k in parts_at(s):
                        if p < NPAIR:
                            qk_part(i, odd, p, which, k)
                        elif more:
                            qk_part(i + 1, 1 - odd, 0, which, k)
                    if more and s in (STEPS + 1, STEPS + 2):
                        v_tile(i + 1, 1 - odd, s - STEPS - 1)
                    if s >= C_LAG:
                        context(i, s - C_LAG)
                for t in range(NT):
                    out_proj(i, t)
                x1_transposes(i, 0)
                if more:
                    v_tile(i + 1, 1 - odd, 2)
                for t in range(1, NT):
                    x1_transposes(i, t)
                if more:
                    v_tile(i + 1, 1 - odd, 3)
                for f in range(FT + 2):
                    if f < FT:
                        ff1(i, f)
                    if f >= 2:
                        ff2(i, f - 2)

            pe.wait_ge(ident_done, 2)
            pe.wait_ge(wl_done, 2)
            for which in range(2):
                for k in range(KT):
                    qk_part(0, 0, 0, which, k)
            pe.wait_ge(wl_done, 3)
            for t in range(NT):
                v_tile(0, 0, t)
            work(0, 0)
            with pe.Fori(1, NBLK - 2, 2) as i:
                work(i, 1)
                work(i + 1, 0)
            work(NBLK - 1, 1, more=False)


_INS = ["x", "x_t", "adj"] + ["L0_gnn_" + n for n in (
    "wq", "bq", "wk", "bk", "wv", "bv", "wo", "bo", "w1", "b1", "w2", "b2", "alpha1", "gamma1", "alpha2", "gamma2")]


def kernel(**inputs):
    import numpy as _np
    import concourse.bacc as _bacc
    from concourse import mybir as _mybir
    from concourse.bass_utils import run_bass_kernel_spmd as _run

    nc = _bacc.Bacc("TRN2", target_bir_lowering=False, num_devices=1, dynamic_dma_scratch_size=1024)
    data = dict(inputs)
    x = _np.ascontiguousarray(inputs["x"])
    data["x_t"] = _np.ascontiguousarray(x.reshape(-1, x.shape[-1]).T)
    arrays, args = {}, []
    for name in _INS:
        a = _np.ascontiguousarray(data[name])
        arrays[f"in_{name}_dram"] = a
        args.append(nc.dram_tensor(f"in_{name}_dram", a.shape, _mybir.dt.from_np(a.dtype), kind="ExternalInput").ap())
    out = nc.dram_tensor("out_0_dram", x.shape, _mybir.dt.from_np(x.dtype), kind="ExternalOutput").ap()
    resnorm_kernel(nc, *args, out)
    r = _run(nc, [arrays], core_ids=[0])
    return r.results[0]["out_0_dram"]
```

```python
from contextlib import ExitStack

import concourse.bass as bass
from concourse import mybir

F32 = mybir.dt.float32
F32R = mybir.dt.float32r
ALU = mybir.AluOpType
ACT = mybir.ActivationFunctionType

P = 128
RMS_EPS = 1e-6
LN_EPS = 1e-5


def resnorm_kernel(nc, x, x_t, adj, wq, bq, wk, bk, wv, bv, wo, bo, w1, b1, w2, b2,
                   alpha1, gamma1, alpha2, gamma2, out):
    B, N, D = x.shape
    F = w1.shape[1]
    H = 8
    DH = D // H
    NPAIR = H // 2
    PW = 64 + DH
    KT = D // P
    FT = F // P
    BPB = 2
    TB = BPB * N
    NT = TB // P
    QT = N // P
    NBLK = B // BPB
    STEPS = H * BPB
    T_LAG, C_LAG = 3, 4
    LAST = STEPS + C_LAG
    TAIL = 14
    W_AT, MEAN_AT, VAR_AT, ROOT_AT, NORM_AT = (3, 4, 7, 8), (3, 4, 7, 8), (6, 7, 10, 11), (5, 6, 9, 10), (8, 9, 12, 13)
    XT_AT = (1, 3, 7)
    SLOTS = T_LAG + 1
    SCALE = float(DH) ** -0.5
    QK0, VP, QKP = 2, NT, 2 * (NPAIR - 1)
    PROJ = QK0 + VP + QKP
    PARTS = (3, 3, 0, 3, 1, 2, 1, 2, 1, 2, 1, 1, 1, 1, 1, 1)
    assert sum(PARTS) == NPAIR * 2 * KT
    assert N == 256 and D == 384 and B % BPB == 0 and PROJ % 2 == 0

    xf = x.rearrange("b n d -> (b n) d")
    outf = out.rearrange("b n d -> (b n) d")
    adj_v = adj.rearrange("b (t p) k -> p (b t) k", p=P)

    with ExitStack() as ctx:
        cursor = [nc.sbuf_base + (-nc.sbuf_base) % 64]

        def put(name, shape, dt=F32, at=None):
            size = 4
            for n in shape[1:]:
                size *= n
            if at is None:
                at = cursor[0]
                cursor[0] += size + (-size) % 32
            return nc.alloc_sbuf_tensor_at(name, shape, dt, offset=at)

        def sem(name):
            return ctx.enter_context(nc.semaphore(name))

        wq_h, wq_l, wk_h, wk_l = [put(n, [P, KT, NPAIR * PW], F32R) for n in ("wq_h", "wq_l", "wk_h", "wk_l")]
        wv_h, wv_l = put("wv_h", [P, KT, D], F32R), put("wv_l", [P, KT, D], F32R)
        wo_h, wo_l = put("wo_h", [P, NPAIR, D], F32R), put("wo_l", [P, NPAIR, D], F32R)
        w1_h, w1_l = put("w1_h", [P, KT, F], F32R), put("w1_l", [P, KT, F], F32R)
        w2_h, w2_l = put("w2_h", [P, FT, D], F32R), put("w2_l", [P, FT, D], F32R)
        bo_bc, gb2_bc, a1_bc, a2_bc, g2_bc = [
            put(n, [P, D]) for n in ("bo_bc", "gb2_bc", "a1_bc", "a2_bc", "g2_bc")]
        ident = put("ident", [P, P])
        nbq, bkc, bvc = put("nbq", [P, NPAIR]), put("bkc", [P, NPAIR]), put("bvc", [P, NPAIR])
        g1c, hb1 = put("g1c", [P, KT]), put("hb1", [P, FT])
        mhalf = put("mhalf", [P, 1])
        nmax, rsum, rrec = [put(n, [P, STEPS * QT]) for n in ("nmax", "rsum", "rrec")]
        ss1, ms1, r1 = [put(n, [P, NT]) for n in ("ss1", "ms1", "r1")]
        ss2, ms2, r2 = [put(n, [P, NT]) for n in ("ss2", "ms2", "r2")]
        sw, nmean, sv, msv, rstd = [put(n, [P, NT]) for n in ("sw", "nmean", "sv", "msv", "rstd")]
        v_h, v_l = put("v_h", [P, NT, D], F32R), put("v_l", [P, NT, D], F32R)
        nadj = put("nadj", [P, NT, N])
        xt_h, xt_l, xt_raw = [], [], []
        over_xt0 = cursor[0]
        for n in range(2):
            xt_h.append(put(f"xt_h{n}", [P, KT, TB], F32R))
            xt_raw.append(put(f"xt_raw{n}", [P, KT, TB], at=cursor[0]))
            xt_l.append(put(f"xt_l{n}", [P, KT, TB], F32R))
        xg_last = put("xg_last", [P, 2, D], at=over_xt0)
        over_x1 = cursor[0]
        x1 = put("x1", [P, NT, D])
        xg = put("xg", [P, 2, D])
        junk = put("junk", [P, D])
        qh0, ql0, kh0, kl0 = [put(n, [P, TB], F32R) for n in ("qh0", "ql0", "kh0", "kl0")]
        over_ctx = cursor[0]
        ctx_h, ctx_l = put("ctx_h", [P, NPAIR, TB], F32R), put("ctx_l", [P, NPAIR, TB], F32R)
        g_h = put("g_h", [P, 4, TB], F32R, at=over_ctx)
        g_l = put("g_l", [P, 4, TB], F32R, at=over_ctx + 4 * TB * 4)
        over_att = cursor[0]
        qh1, ql1, kh1, kl1 = [put(n, [P, TB], F32R) for n in ("qh1", "ql1", "kh1", "kl1")]
        prob = put("prob", [P, SLOTS, QT * N])
        pt_h, pt_l = put("pt_h", [P, 2, TB], F32R), put("pt_l", [P, 2, TB], F32R)
        row = TB * 4
        x1t_h = put("x1t_h", [P, KT, TB], F32R, at=over_att)
        x1t_l = put("x1t_l", [P, KT, TB], F32R, at=over_att + KT * row)
        tnh = put("tnh", [P, 2, TB], at=over_att + 2 * KT * row)
        sil = put("sil", [P, 2, TB], at=over_att + (2 * KT + 2) * row)
        EARLY = 3
        LATE = 2 * D
        stage = [put(f"stage{n}", [P, KT * D], at=over_ctx + n * KT * D * 4) for n in range(EARLY)]
        stage += [put(f"stage_x1{n}", [P, LATE], at=over_x1 + n * LATE * 4) for n in range(2)]
        assert cursor[0] <= nc.sbuf_usable_end
        qh, ql, kh, kl = (qh0, qh1), (ql0, ql1), (kh0, kh1), (kl0, kl1)

        psum = ctx.enter_context(nc.psum_tensor("psum", [P, 8, 512], F32))
        PROJ_BANK, SCORE_BANK, PT_BANK, CTX_BANK = (0, 1), (2, 3), (4, 5), (6, 7)
        WO_BANK = (2, 3, 4, 5)
        X1T_BANK = (6, 7, 2)
        F1_BANK = (3, 2)
        F2_BANK = (4, 5, 6, 7)

        WO_CHUNKS, W1_CHUNKS, W2_CHUNKS = NPAIR // 2, KT * (F // LATE), FT // 2
        NCHUNK = EARLY + WO_CHUNKS + W1_CHUNKS + W2_CHUNKS
        w_in = [sem(f"w_in{n}") for n in range(NCHUNK)]
        qk_bias_in = sem("qk_bias_in")
        const_in = sem("const_in")
        xt_in = [sem(f"xt_in{k}") for k in range(KT)]
        adj_in = sem("adj_in")
        x_in = [sem(f"x_in{t}") for t in range(NT)]
        xg_in = [sem(f"xg_in{t}") for t in range(2)]
        xg_last_in = [sem(f"xg_last_in{t}") for t in range(2)]
        out_dma = [sem(f"out_dma{t}") for t in range(NT)]
        dve_past, pool_past = sem("dve_past"), sem("pool_past")
        zero_done = sem("zero_done")
        bias_done = sem("bias_done")
        const_done = sem("const_done")
        ident_done = sem("ident_done")
        first_hi, first_lo = [sem(f"first_hi{k}") for k in range(KT)], [sem(f"first_lo{k}") for k in range(KT)]
        wh_done = sem("wh_done")
        wl_done = sem("wl_done")
        pool_w_hi = sem("pool_w_hi")
        pool_w_lo = sem("pool_w_lo")
        proj_done = sem("proj_done")
        sc_done = sem("sc_done")
        pt_done = sem("pt_done")
        av_done = sem("av_done")
        wo_done = sem("wo_done")
        x1t_done = sem("x1t_done")
        f1_done = sem("f1_done")
        f2_step = sem("f2_step")
        f2_done = sem("f2_done")
        proj_h = sem("proj_h")
        pt_hi = sem("pt_hi")
        exp_done = sem("exp_done")
        ctx_hi = sem("ctx_hi")
        sq1_done = sem("sq1_done")
        x1t_hi = sem("x1t_hi")
        tz_done = sem("tz_done")
        g_hi = sem("g_hi")
        sq2_done = sem("sq2_done")
        var_done = sem("var_done")
        proj_l = sem("proj_l")
        max_done = sem("max_done")
        rec_done = sem("rec_done")
        pt_lo = sem("pt_lo")
        ctx_lo = sem("ctx_lo")
        t1_done = sem("t1_done")
        x1_done = sem("x1_done")
        x1t_lo = sem("x1t_lo")
        g_done = sem("g_done")
        g_lo = sem("g_lo")
        z_done = sem("z_done")
        w_done = sem("w_done")
        out_done = sem("out_done")
        prob_done = sem("prob_done")
        nadj_done = sem("nadj_done")
        xt_done = sem("xt_done")
        xt_hi = sem("xt_hi")
        x_done = sem("x_done")
        xg_done = sem("xg_done")
        ms1_done = sem("ms1_done")
        r1_done = sem("r1_done")
        x1b_done = sem("x1b_done")
        ms2_done = sem("ms2_done")
        r2_done = sem("r2_done")
        za_done = sem("za_done")
        nmean_done = sem("nmean_done")
        msv_done = sem("msv_done")
        rstd_done = sem("rstd_done")

        def since(eng, semaphore, count):
            if not (isinstance(count, int) and count <= 0):
                eng.wait_ge(semaphore, count)

        def parts_at(s):
            if s >= STEPS:
                return []
            n = sum(PARTS[:s])
            return [(1 + m // (2 * KT), m // KT % 2, m % KT) for m in range(n, n + PARTS[s])]

        def projected_before(s):
            return [(p, which) for p, which, k in parts_at(s - 1) if k == KT - 1] if s > 0 else []

        chunks = [("wq", 0), ("wk", 0), ("wv", 0)] + [("wo", n) for n in range(WO_CHUNKS)] \
            + [("w1", n) for n in range(W1_CHUNKS)] + [("w2", n) for n in range(W2_CHUNKS)]
        WO_WHOLE = EARLY + WO_CHUNKS - 1
        W1_WHOLE = [WO_WHOLE + (k + 1) * (F // LATE) for k in range(KT)]
        W2_WHOLE = [W1_WHOLE[-1] + n + 1 for n in range(W2_CHUNKS)]

        def of_pool(c):
            return c >= EARLY and (c - EARLY) % 2 == 1

        def splits(c):
            by_pool = sum(of_pool(n) for n in range(c + 1))
            return c + 1 - by_pool, by_pool

        def arrivals(c):
            return 32 if chunks[c][0] == "wo" else 16

        def wait_split(eng, c):
            by_dve, by_pool = splits(c)
            eng.wait_ge(wl_done, by_dve)
            if by_pool > 0:
                eng.wait_ge(pool_w_lo, by_pool)

        def stage_of(c):
            return stage[c if c < EARLY else EARLY + (c - EARLY) % 2]

        def chunks_at(s, pool):
            c = EARLY + s - 2 + pool
            return [c] if s >= 2 and s % 2 == 0 and c < NCHUNK else []

        def chunk_parts(c):
            name, n = chunks[c]
            s = stage_of(c)
            if name in ("wq", "wk"):
                h, l = (wq_h, wq_l) if name == "wq" else (wk_h, wk_l)
                parts = []
                for a in range(2):
                    src = s[:, 0:KT * D].rearrange("p (r a d) -> p r a d", a=2, d=DH)[:, :, a, :]
                    dst = [w[:, :, :].rearrange("p k (r c) -> p (k r) c", r=NPAIR)[:, :, 64 * a:64 * a + DH]
                           for w in (h, l)]
                    parts.append((src, *dst))
                return parts
            if name == "wv":
                return [(s[:, 0:KT * D].rearrange("p (k n) -> p k n", k=KT), wv_h[:, :, :], wv_l[:, :, :])]
            if name == "wo":
                v = s[:, :].rearrange("p (r n) -> p r n", r=2)
                return [(v[0:PW], wo_h[0:PW, 2 * n:2 * n + 2, :], wo_l[0:PW, 2 * n:2 * n + 2, :])]
            if name == "w1":
                k, m = divmod(n * LATE, F)
                return [(s[:, :], w1_h[:, k, m:m + LATE], w1_l[:, k, m:m + LATE])]
            v = s[:, :].rearrange("p (g n) -> p g n", g=2)
            return [(v, w2_h[:, 2 * n:2 * n + 2, :], w2_l[:, 2 * n:2 * n + 2, :])]

        pair_biases = [(bq, nbq), (bk, bkc), (bv, bvc)]
        NCONST = 2 + 2 + 6

        block = ctx.enter_context(nc.Block())

        @block.sync
        def _(sp):
            def load_chunk(c):
                name, n = chunks[c]
                s = stage_of(c)
                if c == EARLY:
                    sp.wait_ge(zero_done, 3)
                if c >= EARLY + 2:
                    by_dve, by_pool = splits(c - 2)
                    if of_pool(c - 2):
                        sp.wait_ge(pool_w_lo, by_pool)
                    else:
                        sp.wait_ge(wl_done, by_dve)
                if name in ("wq", "wk", "wv"):
                    w = {"wq": wq, "wk": wk, "wv": wv}[name]
                    sp.dma_start(s[:, 0:KT * D].rearrange("p (k n) -> p k n", k=KT),
                                 w.rearrange("(k p) n -> p k n", p=P)).then_inc(w_in[c], 16)
                elif name == "wo":
                    v = s[:, :].rearrange("p (r n) -> p r n", r=2)
                    src = wo.rearrange("(r a d) n -> a d r n", r=NPAIR, a=2)
                    for a in range(2):
                        sp.dma_start(v[64 * a:64 * a + DH], src[a, :, 2 * n:2 * n + 2, :]).then_inc(w_in[c], 16)
                elif name == "w1":
                    k, m = divmod(n * LATE, F)
                    sp.dma_start(s[:, :], w1[k * P:(k + 1) * P, m:m + LATE]).then_inc(w_in[c], 16)
                else:
                    sp.dma_start(s[:, :].rearrange("p (g n) -> p g n", g=2),
                                 w2[2 * n * P:2 * (n + 1) * P, :].rearrange("(g p) n -> p g n", p=P)
                                 ).then_inc(w_in[c], 16)

            def load_xt(i, odd, k):
                sp.dma_start(xt_raw[odd][:, k, :], x_t[k * P:(k + 1) * P, bass.ds(i * TB, TB)])\
                    .then_inc(xt_in[k], 16)

            def load_adj(i):
                sp.dma_start(nadj[:, :, :], adj_v[:, bass.ds(i * NT, NT), :]).then_inc(adj_in, 16)

            def load_x(dst, i, t, arrived):
                sp.dma_start(dst, xf[bass.ds(i * TB + t * P, P), :]).then_inc(arrived, 16)

            def loads_and_stores(i, odd, tail=True, more=True):
                if more:
                    sp.wait_ge(proj_done, i * PROJ if tail else QK0)
                    for k in range(KT):
                        if tail:
                            sp.wait_ge(xt_done, (i - 1) * KT + k + 1)
                        load_xt(i + 1, 1 - odd, k)
                if tail:
                    j = i - 1
                    for t in range(2):
                        sp.wait_ge(w_done, j * NT + t + 1)
                        load_x(xg[:, t, :], j, t + 2, xg_in[t])
                    for t in range(NT):
                        sp.wait_ge(out_done, j * NT + t + 1)
                        sp.dma_start(outf[bass.ds(j * TB + t * P, P), :], x1[:, t, :]).then_inc(out_dma[t], 16)
                else:
                    for c in range(EARLY, NCHUNK):
                        load_chunk(c)
                    wait_split(sp, NCHUNK - 1)
                for t in range(NT):
                    since(sp, out_dma[t], i * 16)
                    load_x(x1[:, t, :], i, t, x_in[t])
                if more:
                    sp.wait_ge(max_done, i * (STEPS * QT) + STEPS * QT)
                    load_adj(i + 1)
                for t in range(2):
                    since(sp, w_done, i * NT - NT + t + 3)
                    load_x(xg[:, t, :], i, t, xg_in[t])
                if not more:
                    sp.wait_ge(proj_done, i * PROJ)
                    for t in range(2):
                        load_x(xg_last[:, t, :], i, t + 2, xg_last_in[t])

            def load_pair_bias(n, arrived):
                dram, tile = pair_biases[n]
                src = dram.rearrange("(r a d) -> a d r", r=NPAIR, a=2)
                for a in range(2):
                    sp.dma_start(tile[64 * a:64 * a + DH, :], src[a], allow_slow_non_contiguous=True).then_inc(arrived, 16)

            load_xt(0, 0, 0)
            load_chunk(0)
            load_xt(0, 0, 1)
            load_chunk(1)
            load_xt(0, 0, 2)
            sp.wait_ge(zero_done, 1)
            for n in range(2):
                load_pair_bias(n, qk_bias_in)
            load_chunk(2)
            load_pair_bias(2, const_in)
            sp.dma_start(g1c[:, :], gamma1.rearrange("(k p) -> p k", p=P), allow_slow_non_contiguous=True).then_inc(const_in, 16)
            sp.dma_start(hb1[:, :], b1.rearrange("(f p) -> p f", p=P), allow_slow_non_contiguous=True).then_inc(const_in, 16)
            for tile, dram in ((bo_bc, bo), (gb2_bc, gamma1), (a1_bc, alpha1), (a2_bc, alpha2),
                               (g2_bc, gamma2), (junk, b2)):
                sp.dma_start(tile[:, :], dram.partition_broadcast(P)).then_inc(const_in, 16)
            load_adj(0)

            loads_and_stores(0, 0, tail=False)
            with sp.Fori(1, NBLK - 2, 2) as i:
                loads_and_stores(i, 1)
                loads_and_stores(i + 1, 0)
            loads_and_stores(NBLK - 1, 1, more=False)
            j = NBLK - 1
            for t in range(NT):
                sp.wait_ge(out_done, j * NT + t + 1)
                sp.dma_start(outf[j * TB + t * P:j * TB + (t + 1) * P, :], x1[:, t, :]).then_inc(out_dma[t], 16)
            for t in range(NT):
                sp.wait_ge(out_dma[t], 16 * NBLK)

        @block.gpsimd
        def _(pool):
            def split_xt(i, odd, k):
                pool.wait_ge(xt_in[k], i * 16 + 16)
                pool.sem_inc(pool_past, 1)
                raw, high, low = xt_raw[odd][:, k, :], xt_h[odd][:, k, :], xt_l[odd][:, k, :]
                pool.tensor_scalar(high, raw, 1.0, 0.0, ALU.mult, ALU.add).then_inc(xt_hi, 1)
                pool.wait_ge(xt_hi, (i - 1) * KT + k + 1)
                pool.tensor_tensor(low, raw, high.bitcast(F32), ALU.subtract).then_inc(xt_done, 1)

            def first_split(k):
                pool.wait_ge(xt_in[k], 16)
                pool.tensor_scalar(xt_h[0][:, k, :], xt_raw[0][:, k, :], 1.0, 0.0, ALU.mult, ALU.add)\
                    .then_inc(first_hi[k], 1)
                pool.wait_ge(first_hi[k], 1)
                pool.tensor_tensor(xt_l[0][:, k, :], xt_raw[0][:, k, :], xt_h[0][:, k, :].bitcast(F32), ALU.subtract)\
                    .then_inc(first_lo[k], 1)

            def split_weights(c):
                pool.wait_ge(w_in[c], arrivals(c))
                (staged, high, low), = chunk_parts(c)
                pool.tensor_scalar(high, staged, 1.0, 0.0, ALU.mult, ALU.add).then_inc(pool_w_hi, 1)
                pool.wait_ge(pool_w_hi, splits(c)[1])
                pool.tensor_tensor(low, staged, high.bitcast(F32), ALU.subtract).then_inc(pool_w_lo, 1)

            def negate_adj(i):
                pool.wait_ge(adj_in, i * 16 + 16)
                pool.sem_inc(pool_past, 1)
                pool.tensor_scalar(nadj[:, :, :], nadj[:, :, :], -1.0, 0.0, ALU.mult, ALU.add).then_inc(nadj_done, 1)

            def normalise(i, s):
                pool.wait_ge(rec_done, i * STEPS + s + 1)
                pool.sem_inc(pool_past, 1)
                for q in range(QT):
                    c = s * QT + q
                    last = pool.tensor_scalar(prob[:, s % SLOTS, q * N:(q + 1) * N], prob[:, s % SLOTS, q * N:(q + 1) * N],
                                              rrec[:, c:c + 1], 0.0, ALU.mult, ALU.add)
                last.then_inc(prob_done, 1)

            def add_bo(i, t):
                pool.wait_ge(x_in[t], i * 16 + 16)
                pool.tensor_tensor(x1[:, t, :], x1[:, t, :], bo_bc[:, :], ALU.add).then_inc(x_done, 1)

            def add_xg(j, t):
                pool.wait_ge(xg_in[t % 2], j * 32 + 16 * (t // 2) + 16)
                pool.tensor_tensor(xg[:, t % 2, :], xg[:, t % 2, :], g2_bc[:, :], ALU.add).then_inc(xg_done, 1)

            def rsqrt_mean(sums, mean, root, t, eps, mean_done, root_done, count):
                pool.sem_inc(pool_past, 1)
                pool.tensor_scalar(mean[:, t:t + 1], sums[:, t:t + 1], 1.0 / D, eps, ALU.mult, ALU.add)\
                    .then_inc(mean_done, 1)
                pool.wait_ge(mean_done, count)
                pool.tensor_tensor(root[:, t:t + 1], mean[:, t:t + 1], mhalf[:, 0:1], ALU.pow).then_inc(root_done, 1)

            def norm1_root(i, t):
                pool.wait_ge(sq1_done, i * NT + t + 1)
                rsqrt_mean(ss1, ms1, r1, t, RMS_EPS, ms1_done, r1_done, i * NT + t + 1)

            def add_b2(i, t):
                pool.wait_ge(x1t_done, i * KT + KT)
                pool.tensor_tensor(x1[:, t, :], x1[:, t, :], gb2_bc[:, :], ALU.add).then_inc(x1b_done, 1)

            def norm2_root(j, t):
                pool.wait_ge(sq2_done, j * NT + t + 1)
                rsqrt_mean(ss2, ms2, r2, t, RMS_EPS, ms2_done, r2_done, j * NT + t + 1)

            def layer_mean(j, t):
                pool.wait_ge(w_done, j * NT + t + 1)
                pool.sem_inc(pool_past, 1)
                pool.tensor_scalar(nmean[:, t:t + 1], sw[:, t:t + 1], -1.0 / D, 0.0, ALU.mult, ALU.add)\
                    .then_inc(nmean_done, 1)

            def layer_root(j, t):
                pool.wait_ge(var_done, j * NT + t + 1)
                rsqrt_mean(sv, msv, rstd, t, LN_EPS, msv_done, rstd_done, j * NT + t + 1)

            def tail_step(j, s, last=False):
                if s == 0:
                    for t in range(NT):
                        norm2_root(j, t)
                for t in range(NT):
                    if s == MEAN_AT[t]:
                        layer_mean(j, t)
                    if s == ROOT_AT[t]:
                        layer_root(j, t)
                if not last and s in (4, 5):
                    add_xg(j, s - 2)

            def work(i, odd, tail=True, more=True):
                for s in range(STEPS):
                    if tail:
                        tail_step(i - 1, s)
                    normalise(i, s)
                    for c in [] if tail else chunks_at(s, True):
                        split_weights(c)
                    for k in range(KT):
                        if more and s == XT_AT[k]:
                            split_xt(i + 1, 1 - odd, k)
                for t in range(NT):
                    add_bo(i, t)
                for t in range(NT):
                    norm1_root(i, t)
                for t in range(NT):
                    add_b2(i, t)
                if more:
                    negate_adj(i + 1)
                for t in range(2):
                    add_xg(i, t)
                if not more:
                    for t in range(2):
                        pool.wait_ge(xg_last_in[t], 16)
                        pool.tensor_tensor(xg_last[:, t, :], xg_last[:, t, :], g2_bc[:, :], ALU.add).then_inc(xg_done, 1)

            pool.memset(mhalf[:, :], -0.5)
            pool.memset(ident[:, :], 0.0).then_inc(ident_done, 1)
            pool.wait_ge(ident_done, 1)
            pool.affine_select(out=ident[:, :], in_=ident[:, :], compare_op=ALU.not_equal, fill=1.0, base=0,
                               pattern=[[-1, P]], channel_multiplier=1).then_inc(ident_done, 1)
            first_split(0)
            first_split(2)
            pool.wait_ge(qk_bias_in, 4 * 16)
            pool.tensor_scalar(nbq[:, :], nbq[:, :], -SCALE, 0.0, ALU.mult, ALU.add).then_inc(bias_done, 1)
            pool.wait_ge(const_in, 16 * NCONST)
            pool.tensor_scalar(hb1[:, :], hb1[:, :], 0.5, 0.0, ALU.mult, ALU.add)
            pool.tensor_tensor(gb2_bc[:, :], gb2_bc[:, :], junk[:, :], ALU.add).then_inc(const_done, 1)
            negate_adj(0)

            work(0, 0, tail=False)
            with pool.Fori(1, NBLK - 2, 2) as i:
                work(i, 1)
                work(i + 1, 0)
            work(NBLK - 1, 1, more=False)
            for s in range(TAIL):
                tail_step(NBLK - 1, s, last=True)

        @block.scalar
        def _(act):
            def weights_high(c):
                act.wait_ge(w_in[c], arrivals(c))
                for staged, high, _ in chunk_parts(c):
                    last = act.activation(high, staged, ACT.Copy, scale=-SCALE if c == 0 else 1.0)
                last.then_inc(wh_done, 1)

            def proj_high(n, bank, dst, bias=None):
                act.wait_ge(proj_done, n + 1)
                src = psum[0:dst.shape[0], bank, 0:dst.shape[1]]
                if bias is None:
                    act.activation(dst, src, ACT.Copy).then_inc(proj_h, 1)
                else:
                    act.activation(dst, src, ACT.Identity, bias=bias).then_inc(proj_h, 1)

            def qk_high(i, p, which):
                n = i * PROJ + (which if p == 0 else QK0 + VP + 2 * (p - 1) + which)
                since(act, sc_done, i * STEPS + 4 * (p - 1))
                proj_high(n, PROJ_BANK[which], (qh, kh)[which][p % 2][0:PW, :], (nbq, bkc)[which][0:PW, p:p + 1])

            def v_high(i, t):
                since(act, av_done, i * STEPS)
                proj_high(i * PROJ + QK0 + t, PROJ_BANK[t % 2], v_h[:, t, :])

            def exponentials(i, s):
                for q in range(QT):
                    c = s * QT + q
                    act.wait_ge(max_done, i * (STEPS * QT) + c + 1)
                    part = prob[:, s % SLOTS, q * N:(q + 1) * N]
                    act.activation(part, part, ACT.Exp, bias=nmax[:, c:c + 1], scale=-1.0,
                                   accum_out=rsum[:, c:c + 1]).then_inc(exp_done, 1)

            def pt_high(i, s):
                act.wait_ge(pt_done, i * STEPS + s + 1)
                since(act, av_done, i * STEPS + s - 1)
                act.activation(pt_h[:, s % 2, :], psum[:, PT_BANK[s % 2], :], ACT.Copy).then_inc(pt_hi, 1)

            def ctx_high(i, hd):
                p, a = hd // 2, hd % 2
                m = 64 if a == 0 else DH
                act.wait_ge(av_done, i * STEPS + 2 * hd + 2)
                act.activation(ctx_h[64 * a:64 * a + m, p, :], psum[0:m, CTX_BANK[hd % 2], :], ACT.Identity,
                               bias=bvc[64 * a:64 * a + m, p:p + 1]).then_inc(ctx_hi, 1)

            def square1(i, t):
                act.wait_ge(t1_done, i * NT + t + 1)
                act.activation(psum[:, WO_BANK[t], 0:D], x1[:, t, :], ACT.Square,
                               accum_out=ss1[:, t:t + 1]).then_inc(sq1_done, 1)

            def x1t_high(i, k):
                act.wait_ge(x1t_done, i * KT + k + 1)
                act.activation(x1t_h[:, k, :], psum[:, X1T_BANK[k], :], ACT.Identity,
                               bias=g1c[:, k:k + 1]).then_inc(x1t_hi, 1)

            def silu_terms(i, f):
                act.wait_ge(f1_done, i * FT + f + 1)
                if f >= 2:
                    act.wait_ge(g_lo, i * FT + f - 1)
                src = psum[:, F1_BANK[f % 2], :]
                act.activation(tnh[:, f % 2, :], src, ACT.Tanh, bias=hb1[:, f:f + 1], scale=0.5)
                act.activation(sil[:, f % 2, :], src, ACT.Identity, bias=hb1[:, f:f + 1], scale=0.5)\
                    .then_inc(tz_done, 1)

            def hidden_high(i, f):
                act.wait_ge(g_done, i * FT + f + 1)
                if f >= 4:
                    act.wait_ge(f2_step, i * 8 + f - 3)
                act.activation(g_h[:, f % 4, :], sil[:, f % 2, :], ACT.Copy).then_inc(g_hi, 1)

            def square2(j, t):
                act.wait_ge(z_done, j * NT + t + 1)
                act.activation(psum[:, F2_BANK[t], 0:D], x1[:, t, :], ACT.Square,
                               accum_out=ss2[:, t:t + 1]).then_inc(sq2_done, 1)

            def variance(j, t):
                act.wait_ge(nmean_done, j * NT + t + 1)
                since(act, var_done, j * NT + t)
                act.activation(junk[:, :], x1[:, t, :], ACT.Square, bias=nmean[:, t:t + 1],
                               accum_out=sv[:, t:t + 1]).then_inc(var_done, 1)

            def tail_step(j, s):
                if s == 0:
                    for t in range(NT):
                        square2(j, t)
                for t in range(NT):
                    if s == VAR_AT[t]:
                        variance(j, t)

            def work(i, tail=True, more=True):
                for s in range(LAST + 1):
                    if tail:
                        tail_step(i - 1, s)
                    for p, which in projected_before(s):
                        if p < NPAIR:
                            qk_high(i, p, which)
                        elif more:
                            qk_high(i + 1, 0, which)
                    if s >= C_LAG + 2 and (s - C_LAG) % 2 == 0:
                        ctx_high(i, (s - C_LAG - 2) // 2)
                    if T_LAG <= s < STEPS + T_LAG:
                        pt_high(i, s - T_LAG)
                    if s < STEPS:
                        exponentials(i, s)
                    for c in [] if tail else chunks_at(s, False):
                        weights_high(c)
                if more:
                    v_high(i + 1, 0)
                for t in range(NT):
                    square1(i, t)
                if more:
                    v_high(i + 1, 1)
                for k in range(KT):
                    x1t_high(i, k)
                if more:
                    for t in range(2, NT):
                        v_high(i + 1, t)
                for f in range(FT):
                    silu_terms(i, f)
                    hidden_high(i, f)

            act.wait_ge(ident_done, 1)
            act.activation(r1[:, 0:1], mhalf[:, 0:1], ACT.Exp)
            act.wait_ge(zero_done, 2)
            for c in range(EARLY):
                weights_high(c)
                if c == 0:
                    act.wait_ge(xt_in[1], 16)
                    act.activation(xt_h[0][:, 1, :], xt_raw[0][:, 1, :], ACT.Copy).then_inc(first_hi[1], 1)
            act.wait_ge(bias_done, 1)
            for which in range(2):
                qk_high(0, 0, which)
            for t in range(NT):
                v_high(0, t)
            act.wait_ge(const_done, 1)
            work(0, tail=False)
            with act.Fori(1, NBLK - 2, 2) as i:
                work(i)
                work(i + 1)
            work(NBLK - 1, more=False)
            for s in range(TAIL):
                tail_step(NBLK - 1, s)

        @block.vector
        def _(dve):
            def low(dst, src, bias, high, done):
                if bias is None:
                    dve.tensor_tensor(dst, src, high.bitcast(F32), ALU.subtract).then_inc(done, 1)
                else:
                    dve.scalar_tensor_tensor(out=dst, in0=src, scalar=bias, in1=high.bitcast(F32),
                                             op0=ALU.add, op1=ALU.subtract).then_inc(done, 1)

            def weights_low(c):
                dve.wait_ge(wh_done, splits(c)[0])
                for staged, high, lo in chunk_parts(c):
                    if c == 0:
                        last = dve.scalar_tensor_tensor(out=lo, in0=staged, scalar=-SCALE, in1=high.bitcast(F32),
                                                        op0=ALU.mult, op1=ALU.subtract)
                    else:
                        last = dve.tensor_tensor(lo, staged, high.bitcast(F32), ALU.subtract)
                last.then_inc(wl_done, 1)

            def qk_low(i, p, which):
                n = i * PROJ + (which if p == 0 else QK0 + VP + 2 * (p - 1) + which)
                dve.wait_ge(proj_h, n + 1)
                low((ql, kl)[which][p % 2][0:PW, :], psum[0:PW, PROJ_BANK[which], :],
                    (nbq, bkc)[which][0:PW, p:p + 1], (qh, kh)[which][p % 2][0:PW, :], proj_l)

            def v_low(i, t):
                dve.wait_ge(proj_h, i * PROJ + QK0 + t + 1)
                low(v_l[:, t, :], psum[:, PROJ_BANK[t % 2], 0:D], None, v_h[:, t, :], proj_l)

            def maxima(i, s):
                dve.wait_ge(sc_done, i * STEPS + s + 1)
                since(dve, pt_done, i * STEPS + s - SLOTS + 1)
                if s == 0:
                    dve.wait_ge(nadj_done, i + 1)
                dve.sem_inc(dve_past, 1)
                b = s % BPB
                for q in range(QT):
                    c = s * QT + q
                    dve.tensor_tensor_reduce(prob[:, s % SLOTS, q * N:(q + 1) * N],
                                             psum[:, SCORE_BANK[s % 2], q * N:(q + 1) * N],
                                             nadj[:, b * QT + q, :], 1.0, 3.0e38, ALU.add, ALU.min,
                                             nmax[:, c:c + 1]).then_inc(max_done, 1)

            def reciprocals(i, s):
                dve.wait_ge(exp_done, i * (STEPS * QT) + (s + 1) * QT)
                dve.reciprocal(rrec[:, s * QT:(s + 1) * QT], rsum[:, s * QT:(s + 1) * QT]).then_inc(rec_done, 1)

            def pt_low(i, s):
                dve.wait_ge(pt_hi, i * STEPS + s + 1)
                low(pt_l[:, s % 2, :], psum[:, PT_BANK[s % 2], :], None, pt_h[:, s % 2, :], pt_lo)

            def ctx_low(i, hd):
                p, a = hd // 2, hd % 2
                m = 64 if a == 0 else DH
                dve.wait_ge(ctx_hi, i * H + hd + 1)
                low(ctx_l[64 * a:64 * a + m, p, :], psum[0:m, CTX_BANK[hd % 2], :],
                    bvc[64 * a:64 * a + m, p:p + 1], ctx_h[64 * a:64 * a + m, p, :], ctx_lo)

            def residual1(i, t):
                dve.wait_ge(wo_done, i * NT + t + 1)
                dve.wait_ge(x_done, i * NT + t + 1)
                dve.tensor_tensor(x1[:, t, :], psum[:, WO_BANK[t], 0:D], x1[:, t, :], ALU.add).then_inc(t1_done, 1)

            def norm1(i, t):
                dve.wait_ge(r1_done, i * NT + t + 1)
                dve.scalar_tensor_tensor(out=x1[:, t, :], in0=x1[:, t, :], scalar=r1[:, t:t + 1], in1=a1_bc[:, :],
                                         op0=ALU.mult, op1=ALU.mult).then_inc(x1_done, 1)

            def x1t_low(i, k):
                dve.wait_ge(x1t_hi, i * KT + k + 1)
                low(x1t_l[:, k, :], psum[:, X1T_BANK[k], :], g1c[:, k:k + 1], x1t_h[:, k, :], x1t_lo)

            def hidden(i, f):
                dve.wait_ge(tz_done, i * FT + f + 1)
                dve.scalar_tensor_tensor(out=sil[:, f % 2, :], in0=tnh[:, f % 2, :], scalar=1.0, in1=sil[:, f % 2, :],
                                         op0=ALU.add, op1=ALU.mult).then_inc(g_done, 1)
                dve.wait_ge(g_hi, i * FT + f + 1)
                low(g_l[:, f % 4, :], sil[:, f % 2, :], None, g_h[:, f % 4, :], g_lo)

            def residual2(j, t):
                dve.wait_ge(f2_done, j * NT + t + 1)
                dve.wait_ge(x1b_done, j * NT + t + 1)
                dve.tensor_tensor(x1[:, t, :], psum[:, F2_BANK[t], 0:D], x1[:, t, :], ALU.add).then_inc(z_done, 1)

            def times_alpha2(j, t):
                dve.wait_ge(sq2_done, j * NT + t + 1)
                dve.tensor_tensor(x1[:, t, :], x1[:, t, :], a2_bc[:, :], ALU.mult).then_inc(za_done, 1)

            def residual3(j, t, last=False):
                dve.wait_ge(za_done, j * NT + t + 1)
                dve.wait_ge(r2_done, j * NT + t + 1)
                dve.wait_ge(xg_done, j * NT + t + 1)
                dve.scalar_tensor_tensor(out=x1[:, t, :], in0=x1[:, t, :], scalar=r2[:, t:t + 1],
                                         in1=(xg_last if last and t >= 2 else xg)[:, t % 2, :], op0=ALU.mult, op1=ALU.add,
                                         accum_out=sw[:, t:t + 1]).then_inc(w_done, 1)

            def layer_norm(j, t):
                dve.wait_ge(rstd_done, j * NT + t + 1)
                dve.tensor_scalar(x1[:, t, :], x1[:, t, :], nmean[:, t:t + 1], rstd[:, t:t + 1],
                                  ALU.add, ALU.mult).then_inc(out_done, 1)

            def tail_step(j, s):
                if s in (1, 2):
                    times_alpha2(j, 2 * s - 2)
                    times_alpha2(j, 2 * s - 1)
                for t in range(NT):
                    if s == W_AT[t]:
                        residual3(j, t)
                    if s == NORM_AT[t]:
                        layer_norm(j, t)

            def work(i, tail=True, more=True):
                for s in range(LAST + 1):
                    if tail and s == 0:
                        for t in range(NT):
                            residual2(i - 1, t)
                    if s < STEPS:
                        maxima(i, s)
                    for p, which in projected_before(s):
                        if p < NPAIR:
                            qk_low(i, p, which)
                        elif more:
                            qk_low(i + 1, 0, which)
                    if s >= C_LAG + 2 and (s - C_LAG) % 2 == 0:
                        ctx_low(i, (s - C_LAG - 2) // 2)
                    if 1 <= s <= STEPS:
                        reciprocals(i, s - 1)
                    if T_LAG <= s < STEPS + T_LAG:
                        pt_low(i, s - T_LAG)
                    if tail and s > 0:
                        tail_step(i - 1, s)
                    for c in [] if tail else chunks_at(s, False):
                        weights_low(c)
                if more:
                    v_low(i + 1, 0)
                for t in range(NT):
                    residual1(i, t)
                    if t > 0:
                        norm1(i, t - 1)
                if more:
                    v_low(i + 1, 1)
                norm1(i, NT - 1)
                for k in range(KT):
                    x1t_low(i, k)
                if more:
                    for t in range(2, NT):
                        v_low(i + 1, t)
                for f in range(FT):
                    hidden(i, f)

            for w in (nbq, bkc, bvc):
                last = dve.memset(w[:, :], 0.0)
            last.then_inc(zero_done, 1)
            for w in (wq_h, wq_l, wk_h, wk_l):
                gaps = w[:, :, :].rearrange("p k (r c) -> p (k r) c", r=NPAIR)[:, :, DH:64]
                last = dve.memset(gaps.bitcast(F32), 0.0)
            last.then_inc(zero_done, 1)
            for s in stage[EARLY:]:
                last = dve.memset(s[32:64, :], 0.0)
            last.then_inc(zero_done, 1)
            for c in range(EARLY):
                weights_low(c)
                if c == 0:
                    dve.wait_ge(first_hi[1], 1)
                    low(xt_l[0][:, 1, :], xt_raw[0][:, 1, :], None, xt_h[0][:, 1, :], first_lo[1])
            for which in range(2):
                qk_low(0, 0, which)
            for t in range(NT):
                v_low(0, t)
            work(0, tail=False)
            with dve.Fori(1, NBLK - 2, 2) as i:
                work(i)
                work(i + 1)
            work(NBLK - 1, more=False)
            for t in range(NT):
                residual2(NBLK - 1, t)
            j = NBLK - 1
            for t in range(NT):
                times_alpha2(j, t)
            for t in range(NT):
                residual3(j, t, last=True)
            for t in range(NT):
                layer_norm(j, t)

        @block.tensor
        def _(pe):
            def three(o, ah, al, bh, bl, start=True, stop=True):
                pe.matmul(o, ah, bh, start=start, stop=False)
                pe.matmul(o, ah, bl, start=False, stop=False)
                return pe.matmul(o, al, bh, start=False, stop=stop)

            def qk_part(i, odd, p, which, k, first=False):
                n = i * PROJ + (which if p == 0 else QK0 + VP + 2 * (p - 1) + which)
                if k == 0:
                    since(pe, proj_l, n - 1)
                if p == 0 and first:
                    pe.wait_ge(first_lo[k], 1)
                elif p == 0:
                    pe.wait_ge(xt_done, (i - 1) * KT + k + 1)
                wh, wl = ((wq_h, wq_l), (wk_h, wk_l))[which]
                cols = slice(p * PW, (p + 1) * PW)
                last = three(psum[0:PW, PROJ_BANK[which], :], wh[:, k, cols], wl[:, k, cols],
                             xt_h[odd][:, k, :], xt_l[odd][:, k, :], start=(k == 0), stop=(k == KT - 1))
                if k == KT - 1:
                    last.then_inc(proj_done, 1)

            def v_tile(i, odd, t, ks=range(KT)):
                n = i * PROJ + QK0 + t
                if ks[0] == 0:
                    since(pe, proj_l, n - 1)
                tok = slice(t * P, (t + 1) * P)
                for k in ks:
                    last = three(psum[:, PROJ_BANK[t % 2], 0:D], xt_h[odd][:, k, tok], xt_l[odd][:, k, tok],
                                 wv_h[:, k, :], wv_l[:, k, :], start=(k == 0), stop=(k == KT - 1))
                if ks[-1] == KT - 1:
                    last.then_inc(proj_done, 1)

            def scores(i, s):
                p, a, b = s // 4, s // 2 % 2, s % 2
                if s % 4 == 0:
                    pe.wait_ge(proj_l, i * PROJ + (2 if p == 0 else QK0 + VP + 2 * p))
                if s >= 2:
                    pe.wait_ge(max_done, i * (STEPS * QT) + (s - 1) * QT)
                else:
                    since(pe, tz_done, i * FT)
                rows = slice(64 * a, 64 * a + DH)
                for q in range(QT):
                    qs = slice(b * N + q * P, b * N + (q + 1) * P)
                    ks = slice(b * N, (b + 1) * N)
                    last = three(psum[:, SCORE_BANK[s % 2], q * N:(q + 1) * N],
                                 qh[p % 2][rows, qs], ql[p % 2][rows, qs], kh[p % 2][rows, ks], kl[p % 2][rows, ks])
                last.then_inc(sc_done, 1)

            def transposes(i, s):
                pe.wait_ge(prob_done, i * STEPS + s + 1)
                if s >= 2:
                    pe.wait_ge(pt_lo, i * STEPS + s - 1)
                else:
                    since(pe, sq2_done, i * NT - NT + s + 1)
                for kt in range(QT):
                    for q in range(QT):
                        last = pe.transpose(psum[:, PT_BANK[s % 2], kt * N + q * P:kt * N + (q + 1) * P],
                                            prob[:, s % SLOTS, q * N + kt * P:q * N + (kt + 1) * P], ident[:, :])
                last.then_inc(pt_done, 1)

            def context(i, s):
                hd, b = s // 2, s % 2
                m = 64 if hd % 2 == 0 else DH
                if s == 0:
                    pe.wait_ge(proj_l, i * PROJ + QK0 + VP)
                if b == 0:
                    if hd >= 2:
                        pe.wait_ge(ctx_lo, i * H + hd - 1)
                    else:
                        since(pe, sq2_done, i * NT - NT + 3 + hd)
                pe.wait_ge(pt_lo, i * STEPS + s + 1)
                cols = slice(hd * DH, hd * DH + m)
                for kt in range(QT):
                    ps = slice(kt * N, (kt + 1) * N)
                    last = three(psum[0:m, CTX_BANK[hd % 2], b * N:(b + 1) * N],
                                 v_h[:, b * QT + kt, cols], v_l[:, b * QT + kt, cols],
                                 pt_h[:, s % 2, ps], pt_l[:, s % 2, ps], start=(kt == 0), stop=(kt == QT - 1))
                last.then_inc(av_done, 1)

            def out_proj(i, t, pairs):
                if pairs[0] == 0:
                    if t < 2:
                        pe.wait_ge(max_done, i * (STEPS * QT) + (STEPS - 1 + t) * QT)
                    else:
                        pe.wait_ge(pt_lo, i * STEPS + STEPS - 3 + t)
                tok = slice(t * P, (t + 1) * P)
                for p in pairs:
                    if t == 0:
                        pe.wait_ge(ctx_lo, i * H + 2 * (p + 1))
                        wait_split(pe, WO_WHOLE)
                    last = three(psum[:, WO_BANK[t], 0:D], ctx_h[0:PW, p, tok], ctx_l[0:PW, p, tok],
                                 wo_h[0:PW, p, :], wo_l[0:PW, p, :], start=(p == 0), stop=(p == NPAIR - 1))
                if pairs[-1] == NPAIR - 1:
                    last.then_inc(wo_done, 1)

            def x1_transposes(i, t):
                pe.wait_ge(x1_done, i * NT + t + 1)
                if t == 0:
                    pe.wait_ge(sq1_done, i * NT + 1)
                for k in range(KT):
                    last = pe.transpose(psum[:, X1T_BANK[k], t * P:(t + 1) * P],
                                        x1[:, t, k * P:(k + 1) * P], ident[:, :])
                    if t == NT - 1:
                        last.then_inc(x1t_done, 1)

            def ff1(i, f):
                if f == 0:
                    pe.wait_ge(sq1_done, i * NT + 2)
                if f >= 2:
                    pe.wait_ge(tz_done, i * FT + f - 1)
                fs = slice(f * P, (f + 1) * P)
                for k in range(KT):
                    if f == 0:
                        pe.wait_ge(x1t_lo, i * KT + k + 1)
                        wait_split(pe, W1_WHOLE[k])
                    last = three(psum[:, F1_BANK[f % 2], :], w1_h[:, k, fs], w1_l[:, k, fs],
                                 x1t_h[:, k, :], x1t_l[:, k, :], start=(k == 0), stop=(k == KT - 1))
                last.then_inc(f1_done, 1)

            def ff2(i, f):
                pe.wait_ge(g_lo, i * FT + f + 1)
                if f % 2 == 0:
                    wait_split(pe, W2_WHOLE[f // 2])
                for t in range(NT):
                    tok = slice(t * P, (t + 1) * P)
                    last = three(psum[:, F2_BANK[t], 0:D], g_h[:, f % 4, tok], g_l[:, f % 4, tok],
                                 w2_h[:, f, :], w2_l[:, f, :], start=(f == 0), stop=(f == FT - 1))
                    if f == FT - 1:
                        last.then_inc(f2_done, 1)
                if f < 8:
                    last.then_inc(f2_step, 1)

            def work(i, odd, more=True):
                for s in range(STEPS + C_LAG):
                    if s < STEPS:
                        scores(i, s)
                    if T_LAG <= s < STEPS + T_LAG:
                        transposes(i, s - T_LAG)
                    for p, which, k in parts_at(s):
                        if p < NPAIR:
                            qk_part(i, odd, p, which, k)
                        elif more:
                            qk_part(i + 1, 1 - odd, 0, which, k)
                    if more and s in (STEPS, STEPS + 1):
                        v_tile(i + 1, 1 - odd, 0, range(1) if s == STEPS else range(1, KT))
                    if s == LAST - 1:
                        out_proj(i, 0, range(NPAIR - 1))
                    if s >= C_LAG:
                        context(i, s - C_LAG)
                out_proj(i, 1, range(NPAIR - 1))
                out_proj(i, 2, range(1))
                for t in range(NT):
                    out_proj(i, t, (range(3, 4), range(3, 4), range(1, 4), range(4))[t])
                if more:
                    v_tile(i + 1, 1 - odd, 1)
                x1_transposes(i, 0)
                if more:
                    v_tile(i + 1, 1 - odd, 2)
                for t in range(1, NT):
                    x1_transposes(i, t)
                if more:
                    v_tile(i + 1, 1 - odd, 3)
                for f in range(FT + 2):
                    if f < FT:
                        ff1(i, f)
                    if f >= 2:
                        ff2(i, f - 2)

            pe.wait_ge(ident_done, 2)
            for which in range(2):
                pe.wait_ge(wl_done, which + 1)
                for k in range(KT):
                    qk_part(0, 0, 0, which, k, first=True)
            pe.wait_ge(wl_done, 3)
            for t in range(NT):
                v_tile(0, 0, t)
            work(0, 0)
            with pe.Fori(1, NBLK - 2, 2) as i:
                work(i, 1)
                work(i + 1, 0)
            work(NBLK - 1, 1, more=False)


_INS = ["x", "x_t", "adj"] + ["L0_gnn_" + n for n in (
    "wq", "bq", "wk", "bk", "wv", "bv", "wo", "bo", "w1", "b1", "w2", "b2", "alpha1", "gamma1", "alpha2", "gamma2")]


def kernel(**inputs):
    import numpy as _np
    import concourse.bacc as _bacc
    from concourse import mybir as _mybir
    from concourse.bass_utils import run_bass_kernel_spmd as _run

    nc = _bacc.Bacc("TRN2", target_bir_lowering=False, num_devices=1, dynamic_dma_scratch_size=1024)
    data = dict(inputs)
    x = _np.ascontiguousarray(inputs["x"])
    data["x_t"] = _np.ascontiguousarray(x.reshape(-1, x.shape[-1]).T)
    arrays, args = {}, []
    for name in _INS:
        a = _np.ascontiguousarray(data[name])
        arrays[f"in_{name}_dram"] = a
        args.append(nc.dram_tensor(f"in_{name}_dram", a.shape, _mybir.dt.from_np(a.dtype), kind="ExternalInput").ap())
    out = nc.dram_tensor("out_0_dram", x.shape, _mybir.dt.from_np(x.dtype), kind="ExternalOutput").ap()
    resnorm_kernel(nc, *args, out)
    r = _run(nc, [arrays], core_ids=[0])
    return r.results[0]["out_0_dram"]
```
